# Optimizing a Trainium2 kernel written in Bass

```python
import numpy as np
import jax
import jax.numpy as jnp

def _softmax(x, axis=-1):
    return jax.nn.softmax(x, axis=axis)

def _gelu(x):
    return jax.nn.gelu(x, approximate=True)

def _silu(x):
    return jax.nn.silu(x)

def _sigmoid(x):
    return jax.nn.sigmoid(x)

def _layernorm(x, axis=-1, eps=1e-05):
    m = jnp.mean(x, axis=axis, keepdims=True)
    v = jnp.var(x, axis=axis, keepdims=True)
    return (x - m) / jnp.sqrt(v + eps)

def _scatter_add(tgt, idx, src, axis=0):
    return tgt.at[idx].add(src)

def _segment_sum(src, seg, n):
    return jax.ops.segment_sum(src, seg, n)
kernel_name = 'mk_prb_d1_jaxref_r8_1fb0d7'

def setup_inputs(seed: int=0):
    np.random.seed(seed)
    _w = jnp.asarray

    def _L0_attn_setup():
        import math
        import jax, jax.numpy as jnp
        import numpy as np
        H, KV, D = (16, 4, 128)
        HID = 256
        ROPE_BASE = 1000000.0
        EPS = 1e-06

        def _layernorm(x, w, b):
            mu = jnp.mean(x, axis=-1, keepdims=True)
            xc = x - mu
            var = jnp.mean(xc * xc, axis=-1, keepdims=True)
            return xc * jax.lax.rsqrt(var + EPS) * w + b

        def _rope(x, cos, sin):
            xr, xi = (x[..., 0::2], x[..., 1::2])
            c, s = (cos[None, None], sin[None, None])
            out = jnp.stack([xr * c - xi * s, xr * s + xi * c], axis=-1)
            return out.reshape(x.shape)
        key = jax.random.key(seed)
        ks = jax.random.split(key, 3)
        B, S = (2, 256)
        s = 0.02
        return {'x': jax.random.normal(ks[0], (B, S, HID), jnp.float32), 'w_qkv': jax.random.normal(ks[1], (2 * H * D + 2 * KV * D, HID), jnp.float32) * s, 'w_o': jax.random.normal(ks[2], (HID, H * D), jnp.float32) * s, 'q_norm_w': jnp.ones((D,), jnp.float32), 'q_norm_b': jnp.zeros((D,), jnp.float32), 'k_norm_w': jnp.ones((D,), jnp.float32), 'k_norm_b': jnp.zeros((D,), jnp.float32)}
    _L0_attn_in = _L0_attn_setup()

    def _L0_ffn_setup():
        import jax, jax.numpy as jnp
        import numpy as np
        NUM_EXPERTS = 8
        TOP_K = 2
        key = jax.random.key(seed)
        k1, k2, k3, k4 = jax.random.split(key, 4)
        B, T, C, E, D = (4, 256, 256, NUM_EXPERTS, 256)
        scale = 0.02
        return {'x': jax.random.normal(k1, (B, T, C), dtype=jnp.float32), 'w_router': jax.random.normal(k2, (C, E), dtype=jnp.float32) * scale, 'w_fc': jax.random.normal(k3, (E, C, D), dtype=jnp.float32) * scale, 'w_proj': jax.random.normal(k4, (E, D, C), dtype=jnp.float32) * scale}
    _L0_ffn_in = _L0_ffn_setup()
    _d = {'L0_attn_x': _L0_attn_in['x'], 'L0_attn_w_qkv': _L0_attn_in['w_qkv'], 'L0_attn_w_o': _L0_attn_in['w_o'], 'L0_attn_q_norm_w': _L0_attn_in['q_norm_w'], 'L0_attn_q_norm_b': _L0_attn_in['q_norm_b'], 'L0_attn_k_norm_w': _L0_attn_in['k_norm_w'], 'L0_attn_k_norm_b': _L0_attn_in['k_norm_b'], 'L0_ffn_w_router': _L0_ffn_in['w_router'], 'L0_ffn_w_fc': _L0_ffn_in['w_fc'], 'L0_ffn_w_proj': _L0_ffn_in['w_proj']}
    _x0 = _d['L0_attn_x']
    _d['L0_attn_x'] = jax.random.normal(jax.random.fold_in(jax.random.key(seed), 1), (1, 2048, 256), dtype=_x0.dtype)
    del _x0
    return _d

def reference(L0_attn_x, L0_attn_w_qkv, L0_attn_w_o, L0_attn_q_norm_w, L0_attn_q_norm_b, L0_attn_k_norm_w, L0_attn_k_norm_b, L0_ffn_w_router, L0_ffn_w_fc, L0_ffn_w_proj):

    def _L0_attn_ref(x, w_qkv, w_o, q_norm_w, q_norm_b, k_norm_w, k_norm_b):
        import math
        import jax, jax.numpy as jnp
        import numpy as np
        H, KV, D = (16, 4, 128)
        HID = 256
        ROPE_BASE = 1000000.0
        EPS = 1e-06

        def _layernorm(x, w, b):
            mu = jnp.mean(x, axis=-1, keepdims=True)
            xc = x - mu
            var = jnp.mean(xc * xc, axis=-1, keepdims=True)
            return xc * jax.lax.rsqrt(var + EPS) * w + b

        def _rope(x, cos, sin):
            xr, xi = (x[..., 0::2], x[..., 1::2])
            c, s = (cos[None, None], sin[None, None])
            out = jnp.stack([xr * c - xi * s, xr * s + xi * c], axis=-1)
            return out.reshape(x.shape)
        B, S, _ = x.shape
        qkv = x @ w_qkv.T
        qg, k, v = jnp.split(qkv, [2 * H * D, 2 * H * D + KV * D], axis=-1)
        q, gate = jnp.split(qg, 2, axis=-1)
        q = q.reshape(B, S, H, D).transpose(0, 2, 1, 3)
        k = k.reshape(B, S, KV, D).transpose(0, 2, 1, 3)
        v = v.reshape(B, S, KV, D).transpose(0, 2, 1, 3)
        q = _layernorm(q, q_norm_w, q_norm_b)
        k = _layernorm(k, k_norm_w, k_norm_b)
        inv = 1.0 / ROPE_BASE ** (jnp.arange(0, D, 2, dtype=jnp.float32) / D)
        freqs = jnp.outer(jnp.arange(S, dtype=jnp.float32), inv)
        cos, sin = (jnp.cos(freqs), jnp.sin(freqs))
        q = _rope(q, cos, sin)
        k = _rope(k, cos, sin)
        rep = H // KV
        k = jnp.repeat(k, rep, axis=1)
        v = jnp.repeat(v, rep, axis=1)
        scores = jnp.einsum('bhqd,bhkd->bhqk', q, k) / math.sqrt(D)
        causal = jnp.tril(jnp.ones((S, S), bool))
        scores = jnp.where(causal[None, None], scores, -jnp.inf)
        attn = jax.nn.softmax(scores, axis=-1)
        out = jnp.einsum('bhqk,bhkd->bhqd', attn, v)
        out = out.transpose(0, 2, 1, 3).reshape(B, S, H * D)
        out = out * jax.nn.sigmoid(gate)
        return out @ w_o.T

    def _L0_ffn_ref(x, w_router, w_fc, w_proj):
        import jax, jax.numpy as jnp
        import numpy as np
        NUM_EXPERTS = 8
        TOP_K = 2
        B, T, C = x.shape
        E = w_fc.shape[0]
        x_flat = x.reshape(-1, C)
        N = x_flat.shape[0]
        router_logits = x_flat @ w_router
        top_vals, top_idx = jax.lax.top_k(router_logits, TOP_K)
        probs = jax.nn.softmax(top_vals, axis=-1)
        rows = jnp.arange(N)[:, None]
        w_tok = jnp.zeros((N, E), dtype=x.dtype).at[rows, top_idx].add(probs)
        h = jnp.einsum('nc,ecd->ned', x_flat, w_fc)
        h = jnp.square(jax.nn.relu(h))
        y = jnp.einsum('ned,edc->nec', h, w_proj)
        out = jnp.einsum('nec,ne->nc', y, w_tok)
        return out.reshape(B, T, C)
    x = L0_attn_x
    xn = _layernorm(x, axis=-1)
    x = x + _L0_attn_ref(xn, L0_attn_w_qkv, L0_attn_w_o, L0_attn_q_norm_w, L0_attn_q_norm_b, L0_attn_k_norm_w, L0_attn_k_norm_b) + _L0_ffn_ref(xn, L0_ffn_w_router, L0_ffn_w_fc, L0_ffn_w_proj)
    return x

_drawn_inputs = setup_inputs


def setup_inputs(seed=0):
    import zlib

    import numpy as np

    out = dict(_drawn_inputs(seed))
    spreads = {'L0_attn_q_norm_w': (1.0, 0.6),
     'L0_attn_q_norm_b': (0.0, 0.8),
     'L0_attn_k_norm_w': (1.0, 0.6),
     'L0_attn_k_norm_b': (0.0, 0.8)}
    factors = {'L0_attn_w_qkv': 3.611, 'L0_attn_w_o': 3.575}
    for name, (base, spread) in spreads.items():
        noise = np.random.default_rng([zlib.crc32(name.encode()), seed]).standard_normal(out[name].shape)
        drawn = base * np.exp(spread * noise) if base else spread * noise
        out[name] = jnp.asarray(drawn.astype(out[name].dtype))
    for name, factor in factors.items():
        out[name] = (out[name] * factor).astype(out[name].dtype)
    return out
```

```python
from contextlib import ExitStack

import numpy as np

import concourse.bass as bass
from concourse import mybir

F32 = mybir.dt.float32
F32R = mybir.dt.float32r
BF16 = mybir.dt.bfloat16
ALU = mybir.AluOpType
ACT = mybir.ActivationFunctionType
AX = mybir.AxisListType

P = 128
S = 2048
C = 256
D = 128
H = 16
KV = 4
HG = H // KV
E = 8
T = S // P
CT = C // P
CHUNK = 512
ROPE_BASE = 1000000.0
LN_EPS = 1e-5
QK_EPS = 1e-6
MASKED = -3.0e38
NBANK = 5
PT_RING = 3
QW = HG * D
WCOLS = 2 * QW + 2 * D
EG = E // KV
JOBS = EG * (S // CHUNK)


class Steps:

    def __init__(self, sem, per, unit=1):
        self.sem, self.per, self.unit = sem, per, unit

    def after(self, g, n):
        return g * (self.per * self.unit) + (1 + max(n, 0) * self.unit)


def chunks_of(t):
    width = (t + 1) * P
    return [min(CHUNK, width - c) for c in range(0, width, CHUNK)]


def plan_group():
    order, bank_of, prior, number = [], {}, {}, {}
    held = [None] * NBANK
    at = [0]
    fills = [0]
    waiting = []

    def count(kind):
        number[kind] = number.get(kind, 0) + 1
        return number[kind]

    def add(*step):
        number[step] = count(step[0])
        order.append(step)

    def fill(*step):
        b = at[0] % NBANK
        at[0] += 1
        while held[b] is not None and held[b][0] == "S" and ("exp", *held[b][1:]) not in number:
            add("exp", *waiting.pop(0))
        fills[0] += 1
        bank_of[step], prior[step], held[b] = b, held[b], step
        number[("fill", step)] = fills[0]
        number[step] = count(step[0])

    def project(t):
        for part in ("Q", "KV", "G"):
            fill(part, t)
        add("project", t)

    def expert_up(m):
        fill("H", m, 0)
        fill("H", m, 1)
        add("expert_up", m)

    def expert_down(m):
        fill("Y", m, 0)
        fill("Y", m, 1)
        add("expert_down", m)

    def turn_qk(t):
        fill("QT", t)
        fill("KT", t)
        add("turn_qk", t)

    def turn_gate(t):
        fill("GT", t)
        add("turn_gate", t)

    def project_out(t):
        fill("OUT", t)
        add("project_out", t)

    def scores(t, h, c):
        fill("S", t, h, c)
        add("scores", t, h, c)
        if c == len(chunks_of(t)) - 1:
            waiting.extend((t, h, i) for i in range(c + 1))

    def exps(n):
        for _ in range(min(n, len(waiting))):
            add("exp", *waiting.pop(0))

    units = [(t, p) for t in range(T) for p in range(HG // 2)]
    pending_pv = []

    def flush_pv(keep):
        while len(pending_pv) > keep:
            add("pv", *pending_pv.pop(0))

    add("split_weights")
    expert_up(0)
    project(0)
    expert_down(0)
    expert_up(1)
    turn_qk(0)
    expert_down(1)
    for h in range(2):
        scores(0, h, 0)
    job = 2
    for n, (t, p) in enumerate(units):
        jps = (t + 2) // 2
        todo = []
        if n + 1 < len(units):
            t1, p1 = units[n + 1]
            todo = [(t1, 2 * p1 + hh, c) for hh in range(2) for c in range(len(chunks_of(t1)))]
        total = len(todo)
        if p == 1 and t + 1 < T:
            turn_qk(t + 1)
        with_job = job < JOBS
        for i in range(jps):
            while any((t, 2 * p + hh, (2 * i + 1) // 4) in waiting or (t, 2 * p + hh, (2 * i) // 4) in waiting
                      for hh in range(2)):
                exps(1)
            add("turn_probs", t, p, i)
            while todo and (total - len(todo)) * max(1, jps - 1) < total * (i + 1):
                scores(*todo.pop(0))
            exps(2)
            flush_pv(1)
            pending_pv.append((t, p, i))
            if i == min(1, jps - 1):
                while todo and todo[0][2] > 0:
                    scores(*todo.pop(0))
                if with_job:
                    expert_up(job)
                if p == 0:
                    if t > 0:
                        flush_pv(len([x for x in pending_pv if x[0] == t]))
                        turn_gate(t - 1)
                    if t + 1 < T:
                        project(t + 1)
                    if t > 0:
                        project_out(t - 1)
        while todo:
            scores(*todo.pop(0))
        if with_job:
            expert_down(job)
            job += 1
    flush_pv(0)
    turn_gate(T - 1)
    project_out(T - 1)
    return order, bank_of, prior, number


def build(nc, x, w_in, w_o, q_w, q_b, k_w, k_b, w_router, w_fc, w_proj, cos, sin, ident, mask, out):
    order, bank_of, prior, number = plan_group()

    def total(kind):
        return number.get(kind, 0)

    with ExitStack() as ctx:
        def sb(name, shape, dt=F32):
            return ctx.enter_context(nc.sbuf_tensor(name, shape, dt))

        def sem(name):
            return ctx.enter_context(nc.semaphore(name))

        acc = sb("acc", [P, T, C])
        xT_hi = sb("xT_hi", [P, CT, S], F32R)
        xT_lo = sb("xT_lo", [P, CT, S], F32R)
        w_raw = sb("w_raw", [P, WCOLS])
        w_hi = sb("w_hi", [P, CT, WCOLS], F32R)
        w_lo = sb("w_lo", [P, CT, WCOLS], F32R)
        kT_hi = sb("kT_hi", [P, S], F32R)
        kT_lo = sb("kT_lo", [P, S], F32R)
        v_hi = sb("v_hi", [P, T, D], F32R)
        v_lo = sb("v_lo", [P, T, D], F32R)
        cos_sb = sb("cos_sb", [P, T, D // 2])
        sin_sb = sb("sin_sb", [P, T, D // 2])
        probs = sb("probs", [P, 2, 2, S])
        wo_sb = sb("wo_sb", [P, HG, C])
        qT_hi = sb("qT_hi", [P, QW], F32R)
        qT_lo = sb("qT_lo", [P, QW], F32R)
        pT_hi = sb("pT_hi", [P, PT_RING, CHUNK], F32R)
        pT_lo = sb("pT_lo", [P, PT_RING, CHUNK], F32R)
        qk_raw = sb("qk_raw", [P, HG + 1, D])
        squares = sb("squares", [P, HG + 1, D])
        rotated = squares
        t_same = sb("t_same", [P, HG + 1, D])
        t_swap = sb("t_swap", [P, HG + 1, D])
        table_same = sb("table_same", [P, 2, D])
        table_swap = sb("table_swap", [P, 2, D])
        table_bias = sb("table_bias", [P, 2, D])
        bias_part = t_swap[:, 0:2, :]
        gate = sb("gate", [P, 2, QW])
        oT = sb("oT", [P, QW])
        ogT = sb("ogT", [P, QW])
        fc_raw = sb("fc_raw", [P, CT, C])
        fc_hi = sb("fc_hi", [P, CT, C], F32R)
        fc_lo = sb("fc_lo", [P, CT, C], F32R)
        pj_sb = sb("pj_sb", [P, CT, C])
        hidden = sb("hidden", [P, 2, CHUNK])
        ident_f = sb("ident_f", [P, P])
        ident_b = sb("ident_b", [P, P], BF16)
        mask_b = sb("mask_b", [P, P], BF16)
        ln_w = sb("ln_w", [P, 2, D])
        ln_b = sb("ln_b", [P, 2, D])
        ln_ws = sb("ln_ws", [P, 2, D])
        ln_bs = sb("ln_bs", [P, 2, D])
        head_sum = sb("head_sum", [P, HG + 1])
        head_mean = sb("head_mean", [P, HG + 1])
        sumsq = sb("sumsq", [P, HG + 1])
        variance = sb("variance", [P, HG + 1])
        rstd = sb("rstd", [P, HG + 1])
        minus_half = sb("minus_half", [P, T])
        neg_chunk_max = sb("neg_chunk_max", [P, 2, 2, 4])
        neg_max = sb("neg_max", [P, 2, 2])
        chunk_sum = sb("chunk_sum", [P, 2, HG, 4])
        row_sum = sb("row_sum", [P, HG])
        twice_sum = sb("twice_sum", [P, HG])
        half_inv = sb("half_inv", [P, HG])
        wr_hi = sb("wr_hi", [P, CT, E], F32R)
        wr_lo = sb("wr_lo", [P, CT, E], F32R)
        w_tok = sb("w_tok", [P, E, T])
        w_tok_g = sb("w_tok_g", [P, EG, T])
        xn = probs[:, 0, :, :].rearrange("p a (t c) -> p (a t) c", c=C)
        rt = [probs[:, 1, 0, i * T * E:(i + 1) * T * E].rearrange("p (t e) -> p t e", e=E) for i in range(4)]
        x_stats = probs[:, 1, 1, 0:T * 6].rearrange("p (t s) -> p t s", s=6)
        x_mv = probs[:, 1, 1, 128:128 + 2 * T].rearrange("p (t s) -> p t s", s=2)
        x_var = probs[:, 1, 1, 192:192 + T]
        x_rstd = probs[:, 1, 1, 224:224 + T]
        rank = probs[:, 1, 1, 256:256 + E]
        wr_raw = probs[:, 1, 1, 288:288 + CT * E].rearrange("p (a e) -> p a e", e=E)
        rs = [probs[:, 1, 1, 320 + 32 * i:320 + 32 * i + T] for i in range(6)]
        mask_f = hidden[:, 0, 0:P]

        banks = [ctx.enter_context(nc.psum_tensor(f"bank{b}", [P, CHUNK], F32)) for b in range(NBANK)]
        pt_bank = [ctx.enter_context(nc.psum_tensor(f"pt_bank{b}", [P, CHUNK], F32)) for b in range(2)]
        o_bank = ctx.enter_context(nc.psum_tensor("o_bank", [P, CHUNK], F32))

        def bank(*step):
            return banks[bank_of[step]]

        x_in, tables_in, consts_in = sem("x_in"), sem("tables_in"), sem("consts_in")
        pre_dve, pre_pool, pre_act, pre_pe = sem("pre_dve"), sem("pre_pool"), sem("pre_act"), sem("pre_pe")
        stored = sem("stored")

        filled = Steps(sem("filled"), len(bank_of))
        pt_filled = Steps(sem("pt_filled"), total("turn_probs"))
        pv_done = Steps(sem("pv_done"), total("pv"))
        w_in_sem = Steps(sem("w_loaded"), CT, 16)
        wo_in = Steps(sem("wo_loaded"), 1, 16)
        fc_in = Steps(sem("fc_loaded"), EG, 16)
        pj_in = Steps(sem("pj_loaded"), EG, 16)
        mean_step = Steps(sem("mean_step"), 3 * CT)
        w_hi_done = Steps(sem("w_hi_done"), CT)
        w_lo_done = Steps(sem("w_lo_done"), CT)
        fc_hi_done = Steps(sem("fc_hi_done"), EG)
        fc_lo_done = Steps(sem("fc_lo_done"), EG)
        wtok_done = Steps(sem("wtok_done"), 1)
        qkv_read = Steps(sem("qkv_read"), 3 * T)
        v_lo_done = Steps(sem("v_lo_done"), T)
        gate_done = Steps(sem("gate_done"), T)
        sumsq_done = Steps(sem("sumsq_done"), T)
        variance_done = Steps(sem("variance_done"), T)
        rstd_done = Steps(sem("rstd_done"), T)
        bias_parts = Steps(sem("bias_parts"), T)
        tables_done = Steps(sem("tables_done"), T)
        same_done = Steps(sem("same_done"), T)
        swap_done = Steps(sem("swap_done"), T)
        both_done = Steps(sem("both_done"), T)
        rotated_done = Steps(sem("rotated_done"), T)
        qk_hi_done = Steps(sem("qk_hi_done"), 2 * T)
        qk_lo_done = Steps(sem("qk_lo_done"), 2 * T)
        n_chunks = total("scores")
        chunk_max_done = Steps(sem("chunk_max_done"), n_chunks)
        neg_max_done = Steps(sem("neg_max_done"), T * HG)
        exp_done = Steps(sem("exp_done"), n_chunks)
        pt_hi_done = Steps(sem("pt_hi_done"), total("turn_probs"))
        pt_lo_done = Steps(sem("pt_lo_done"), total("turn_probs"))
        o_copied = Steps(sem("o_copied"), T * HG // 2)
        sum_step = Steps(sem("sum_step"), 2 * T)
        inv_done = Steps(sem("inv_done"), T)
        gated = Steps(sem("gated"), T)
        og_done = Steps(sem("og_done"), T)
        relu_done = Steps(sem("relu_done"), 2 * JOBS)
        hidden_done = Steps(sem("hidden_done"), JOBS)
        acc_done = Steps(sem("acc_done"), T + 4 * JOBS)

        freed_by = {
            "Q": lambda t: (qkv_read, 3 * t + 1),
            "KV": lambda t: (v_lo_done, t + 1),
            "G": lambda t: (gate_done, t + 1),
            "QT": lambda t: (qk_lo_done, 2 * t + 1),
            "KT": lambda t: (qk_lo_done, 2 * t + 2),
            "GT": lambda t: (og_done, t + 1),
            "OUT": lambda t: (acc_done, acc_number["OUT", t]),
            "S": lambda t, h, c: (exp_done, number["exp", t, h, c]),
            "H": lambda m, d: (relu_done, 2 * m + d + 1),
            "Y": lambda m, half: (acc_done, acc_number["Y", m, half]),
        }
        acc_number, acc_before, last_add, adds = {}, {}, {}, 0
        for step in order:
            if step[0] == "project_out":
                adds += 1
                acc_number["OUT", step[1]] = adds
                acc_before[adds] = last_add.get(step[1], 0)
                last_add[step[1]] = adds
            if step[0] == "expert_down":
                for half in range(2):
                    for k in range(2):
                        adds += 1
                        tile = (step[1] % 4) * 4 + 2 * half + k
                        acc_before[adds] = last_add.get(tile, 0)
                        last_add[tile] = adds
                    acc_number["Y", step[1], half] = adds
        last_fill = [None] * NBANK
        for step, b in bank_of.items():
            last_fill[b] = step

        def wait(eng, steps, g, n):
            eng.wait_ge(steps.sem, steps.after(g, n))

        def wait_bank_free(eng, g, *step):
            before = prior[step]
            if before is None:
                s, _ = freed_by[last_fill[bank_of[step]][0]](*last_fill[bank_of[step]][1:])
                wait(eng, s, g, 0)
            else:
                s, n = freed_by[before[0]](*before[1:])
                wait(eng, s, g, n)

        def wait_filled(eng, g, *step):
            wait(eng, filled, g, number["fill", step])

        block = ctx.enter_context(nc.Block())

        @block.sync
        def _(sp):
            x_tiles = x.rearrange("(t p) c -> p t c", p=P)
            for q in range(4):
                sp.dma_start(acc[:, 4 * q:4 * q + 4, :], x_tiles[:, 4 * q:4 * q + 4, :]).then_inc(x_in, 16)
            sp.dma_start(ident_f[:], ident).then_inc(consts_in, 16)
            sp.dma_start(mask_f, mask).then_inc(consts_in, 16)
            sp.dma_start(wr_raw, w_router.rearrange("(a p) e -> p a e", p=P)).then_inc(consts_in, 16)
            for i, v in enumerate((q_w, k_w)):
                sp.dma_start(ln_w[:, i, :], v.partition_broadcast(P)).then_inc(tables_in, 16)
            for i, v in enumerate((q_b, k_b)):
                sp.dma_start(ln_b[:, i, :], v.partition_broadcast(P)).then_inc(tables_in, 16)
            sp.dma_start(cos_sb[:], cos.rearrange("(t p) d -> p t d", p=P)).then_inc(tables_in, 16)
            sp.dma_start(sin_sb[:], sin.rearrange("(t p) d -> p t d", p=P)).then_inc(tables_in, 16)
            for s in (w_in_sem, wo_in, fc_in, pj_in):
                sp.sem_inc(s.sem, 1)
            with sp.Fori(0, KV) as g:
                for a in range(CT):
                    if a == 0:
                        wait(sp, w_hi_done, g, 0)
                        wait(sp, w_lo_done, g, 0)
                    else:
                        wait(sp, w_hi_done, g, a)
                        wait(sp, w_lo_done, g, a)
                    sp.dma_start(w_raw[:], w_in[bass.ds(g, 1), a]
                                 .rearrange("o p n -> p (o n)")).then_inc(w_in_sem.sem, 16)
                wait(sp, filled, g, 0)
                for e in range(EG):
                    if e == 0:
                        wait(sp, fc_lo_done, g, 0)
                        wait(sp, fc_hi_done, g, 0)
                    else:
                        wait(sp, fc_lo_done, g, e)
                        wait(sp, fc_hi_done, g, e)
                    sp.dma_start(fc_raw[:], w_fc[bass.ds(g, 1), e]
                                 .rearrange("o (a p) n -> p (o a) n", p=P)).then_inc(fc_in.sem, 16)
                    if e == 0:
                        sp.dma_start(wo_sb[:], w_o[bass.ds(g, 1)]
                                     .rearrange("o (h p) n -> p (o h) n", p=P)).then_inc(wo_in.sem, 16)
                    else:
                        wait(sp, filled, g, number["fill", ("Y", 4 * e - 1, 1)])
                    sp.dma_start(pj_sb[:], w_proj[bass.ds(g, 1), e]
                                 .rearrange("o (a p) n -> p (o a) n", p=P)).then_inc(pj_in.sem, 16)
            out_tiles = out.rearrange("(t p) c -> p t c", p=P)
            sp.wait_ge(acc_done.sem, 1 + KV * acc_done.per)
            for q in range(4):
                sp.dma_start(out_tiles[:, 4 * q:4 * q + 4, :], acc[:, 4 * q:4 * q + 4, :]).then_inc(stored, 16)
            sp.wait_ge(stored, 64)

        @block.gpsimd
        def _(pool):
            for s in (rstd_done, bias_parts, tables_done, swap_done):
                pool.sem_inc(s.sem, 1)
            pool.memset(minus_half[:], -0.5).then_inc(pre_pool, 1)
            for e in range(E):
                pool.memset(rank[:, e:e + 1], float(E - e)).then_inc(pre_pool, 1)
            pool.wait_ge(pre_pool, 1 + E)
            pool.wait_ge(pre_dve, 2 * T)
            pool.tensor_scalar(x_var, x_mv[:, :, 1], LN_EPS, None, ALU.add).then_inc(pre_pool, 1)
            pool.wait_ge(pre_pool, 2 + E)
            pool.tensor_tensor(x_rstd, x_var, minus_half[:], ALU.pow).then_inc(pre_pool, 1)
            pool.wait_ge(tables_in, 96)
            pool.tensor_scalar(ln_w[:, 0, :], ln_w[:, 0, :], D ** -0.5, None, ALU.mult).then_inc(pre_pool, 1)
            pool.tensor_scalar(ln_b[:, 0, :], ln_b[:, 0, :], D ** -0.5, None, ALU.mult).then_inc(pre_pool, 1)
            pool.wait_ge(pre_pool, 5 + E)
            for full, swapped in ((ln_w, ln_ws), (ln_b, ln_bs)):
                pool.tensor_scalar(swapped[:, :, 0:64], full[:, :, 64:128], -1.0, None, ALU.mult)
                pool.tensor_scalar(swapped[:, :, 64:128], full[:, :, 0:64], 1.0, None, ALU.mult)\
                    .then_inc(pre_pool, 1)
            pool.wait_ge(pre_pool, 7 + E)

            def halves(ap):
                return ap.rearrange("p a (b d) -> p (a b) d", b=2)

            def tables(g, t):
                cos_t = cos_sb[:, t:t + 1, :].to_broadcast([P, 4, D // 2])
                sin_t = sin_sb[:, t:t + 1, :].to_broadcast([P, 4, D // 2])
                wait(pool, same_done, g, t)
                wait(pool, swap_done, g, t)
                wait(pool, rotated_done, g, t)
                pool.tensor_tensor(halves(table_same[:]), halves(ln_w[:]), cos_t, ALU.mult)
                pool.tensor_tensor(halves(table_swap[:]), halves(ln_ws[:]), sin_t, ALU.mult)
                pool.tensor_tensor(halves(table_bias[:]), halves(ln_b[:]), cos_t, ALU.mult)
                pool.tensor_tensor(halves(bias_part), halves(ln_bs[:]), sin_t, ALU.mult)\
                    .then_inc(bias_parts.sem, 1)
                wait(pool, bias_parts, g, t + 1)
                pool.tensor_tensor(table_bias[:], table_bias[:], bias_part, ALU.add)\
                    .then_inc(tables_done.sem, 1)

            with pool.Fori(0, KV) as g:
                tables(g, 0)
                for step in order:
                    if step[0] == "project":
                        t = step[1]
                        wait(pool, qkv_read, g, 3 * t + 2)
                        wait(pool, tables_done, g, t + 1)
                        for heads, i in ((slice(0, HG), 0), (slice(HG, HG + 1), 1)):
                            n = heads.stop - heads.start
                            for a, b in ((slice(0, 64), slice(64, 128)), (slice(64, 128), slice(0, 64))):
                                ins = pool.tensor_tensor(
                                    t_swap[:, heads, a], qk_raw[:, heads, b],
                                    table_swap[:, i:i + 1, a].to_broadcast([P, n, 64]), ALU.mult)
                        ins.then_inc(swap_done.sem, 1)
                        wait(pool, variance_done, g, t + 1)
                        wait(pool, rotated_done, g, t)
                        pool.tensor_tensor(rstd[:], variance[:], minus_half[:, 0:HG + 1], ALU.pow)\
                            .then_inc(rstd_done.sem, 1)
                        if t + 1 < T:
                            tables(g, t + 1)

        @block.scalar
        def _(act):
            for s in (w_hi_done, fc_hi_done, qkv_read, gate_done, qk_hi_done, exp_done, pt_hi_done,
                      o_copied, relu_done, hidden_done, gated):
                act.sem_inc(s.sem, 1)
            act.wait_ge(consts_in, 48)
            act.activation(wr_hi[:], wr_raw, ACT.Copy).then_inc(pre_act, 1)
            act.activation(ident_b[:], ident_f[:], ACT.Copy).then_inc(pre_act, 1)
            act.activation(mask_b[:], mask_f, ACT.Copy).then_inc(pre_act, 1)
            for i in range(CT * 4):
                act.wait_ge(pre_pe, i + 1)
                act.activation(xT_hi[:, i % 2, (i // 2) * CHUNK:(i // 2 + 1) * CHUNK], banks[i % 4][:],
                               ACT.Copy).then_inc(pre_act, 1)
            act.wait_ge(pre_dve, 3 * T + 1 + 8 + 10)
            act.activation(rs[3], rs[2], ACT.Exp).then_inc(pre_act, 1)

            with act.Fori(0, KV) as g:
                for step in order:
                    kind, a = step[0], step[1:]
                    if kind == "split_weights":
                        for c in range(CT):
                            wait(act, mean_step, g, 3 * c + 3)
                            wait(act, filled, g, 0)
                            act.activation(w_hi[:, c, :], w_raw[:], ACT.Copy).then_inc(w_hi_done.sem, 1)
                    elif kind == "expert_up":
                        m = a[0]
                        if m % 4 == 0:
                            e = m // 4
                            wait(act, fc_in, g, e + 1)
                            wait(act, filled, g, number["fill", ("H", m - 1, 1)] if m else 0)
                            act.activation(fc_hi[:], fc_raw[:], ACT.Copy).then_inc(fc_hi_done.sem, 1)
                        for d in range(2):
                            wait_filled(act, g, "H", m, d)
                            if d == 0:
                                wait(act, filled, g, number["fill", ("Y", m - 1, 1)] if m else 0)
                            act.activation(hidden[:, d, :], bank("H", m, d)[:], ACT.Relu)\
                                .then_inc(relu_done.sem, 1)
                        wait(act, relu_done, g, 2 * m + 2)
                        act.activation(hidden[:], hidden[:], ACT.Square).then_inc(hidden_done.sem, 1)
                    elif kind == "project":
                        t = a[0]
                        wait_filled(act, g, "Q", t)
                        wait(act, same_done, g, t)
                        wait(act, swap_done, g, t)
                        wait(act, filled, g, number["fill", ("KT", t - 1)] if t else 0)
                        act.activation(qk_raw[:, 0:HG, :], bank("Q", t)[:], ACT.Copy)
                        act.activation(squares[:, 0:HG, :], bank("Q", t)[:], ACT.Square)\
                            .then_inc(qkv_read.sem, 1)
                        wait_filled(act, g, "KV", t)
                        act.activation(qk_raw[:, HG, :], bank("KV", t)[:, 0:D], ACT.Copy)
                        act.activation(squares[:, HG, :], bank("KV", t)[:, 0:D], ACT.Square)\
                            .then_inc(qkv_read.sem, 1)
                        act.activation(v_hi[:, t, :], bank("KV", t)[:, D:2 * D], ACT.Copy)\
                            .then_inc(qkv_read.sem, 1)
                        wait_filled(act, g, "G", t)
                        wait(act, filled, g, number["fill", ("GT", t - 2)] if t >= 2 else 0)
                        act.activation(gate[:, t % 2, :], bank("G", t)[:], ACT.Tanh, scale=0.5)\
                            .then_inc(gate_done.sem, 1)
                    elif kind == "turn_qk":
                        t = a[0]
                        wait_filled(act, g, "QT", t)
                        act.activation(qT_hi[:], bank("QT", t)[:], ACT.Copy).then_inc(qk_hi_done.sem, 1)
                        wait_filled(act, g, "KT", t)
                        act.activation(kT_hi[:, t * P:(t + 1) * P], bank("KT", t)[:, 0:P], ACT.Copy)\
                            .then_inc(qk_hi_done.sem, 1)
                    elif kind == "exp":
                        t, h, c = a
                        u, w = (2 * t + h // 2) % 2, chunks_of(t)[c]
                        wait(act, neg_max_done, g, HG * t + h + 1)
                        act.activation(probs[:, u, h % 2, c * CHUNK:c * CHUNK + w], bank("S", t, h, c)[:, 0:w],
                                       ACT.Exp, bias=neg_max[:, u, h % 2:h % 2 + 1],
                                       accum_out=chunk_sum[:, t % 2, h, c:c + 1]).then_inc(exp_done.sem, 1)
                    elif kind == "turn_gate":
                        t = a[0]
                        wait(act, inv_done, g, t + 1)
                        wait(act, gate_done, g, t + 1)
                        for h in range(HG):
                            gh, inv = gate[:, t % 2, h * D:(h + 1) * D], half_inv[:, h:h + 1]
                            ins = act.activation(gh, gh, ACT.Identity, bias=inv, scale=inv)
                        ins.then_inc(gated.sem, 1)
                    elif kind == "turn_probs":
                        t, p, i = a
                        n = number[step]
                        w = 256 * min(2, t + 1 - 2 * i)
                        wait(act, pt_filled, g, n)
                        wait(act, pv_done, g, n - PT_RING)
                        act.activation(pT_hi[:, n % PT_RING, 0:w], pt_bank[n % 2][:, 0:w], ACT.Copy)\
                            .then_inc(pt_hi_done.sem, 1)
                    elif kind == "pv" and a[2] == (a[0] + 2) // 2 - 1:
                        t, p, i = a
                        wait(act, pv_done, g, number[step])
                        wait(act, og_done, g, t)
                        act.activation(oT[:, 256 * p:256 * p + 256], o_bank[:, 256 * p:256 * p + 256],
                                       ACT.Copy).then_inc(o_copied.sem, 1)

        @block.vector
        def _(dve):
            for s in (mean_step, variance_done, w_lo_done, fc_lo_done, wtok_done, v_lo_done, sumsq_done, same_done, both_done,
                      rotated_done, qk_lo_done, chunk_max_done, neg_max_done, pt_lo_done, sum_step, inv_done,
                      og_done, acc_done):
                dve.sem_inc(s.sem, 1)
            for t in range(T):
                dve.wait_ge(x_in, 16 * 4)
                dve.bn_stats(x_stats[:, t, :], acc[:, t, :]).then_inc(pre_dve, 1)
            for t in range(T):
                dve.wait_ge(pre_dve, t + 1)
                dve.bn_aggr(x_mv[:, t, :], x_stats[:, t, :]).then_inc(pre_dve, 1)
            dve.wait_ge(pre_pool, 3 + E)
            dve.wait_ge(pre_dve, 2 * T)
            for t in range(T):
                dve.tensor_scalar(xn[:, t, :], acc[:, t, :], x_mv[:, t, 0:1], x_rstd[:, t:t + 1],
                                  ALU.subtract, ALU.mult).then_inc(pre_dve, 1)
            dve.wait_ge(pre_act, 1)
            dve.tensor_tensor(wr_lo[:], wr_raw, wr_hi[:].bitcast(F32), ALU.subtract).then_inc(pre_dve, 1)
            for i in range(CT * 4):
                dve.wait_ge(pre_act, 3 + i + 1)
                cols = slice((i // 2) * CHUNK, (i // 2 + 1) * CHUNK)
                dve.tensor_tensor(xT_lo[:, i % 2, cols], banks[i % 4][:], xT_hi[:, i % 2, cols].bitcast(F32),
                                  ALU.subtract).then_inc(pre_dve, 1)
            n0 = 3 * T + 1 + CT * 4
            logit, pick0, rest, pick1 = rt
            top0, r_a, diff, ex, p1, p0 = rs
            done = n0

            def link(ins):
                nonlocal done
                done += 1
                ins.then_inc(pre_dve, 1)
                dve.wait_ge(pre_dve, done)

            def over_experts(ap):
                return ap.unsqueeze(2).to_broadcast([P, T, E])

            rank_all = rank.unsqueeze(1).to_broadcast([P, T, E])
            dve.wait_ge(pre_pe, CT * 4 + 1)
            link(dve.tensor_copy(logit.rearrange("p t e -> p (t e)"), banks[4][:, 0:T * E]))
            link(dve.tensor_reduce(top0, logit, AX.X, ALU.max))
            link(dve.tensor_tensor(rest, logit, over_experts(top0), ALU.is_equal))
            link(dve.tensor_tensor(rest, rest, rank_all, ALU.mult))
            link(dve.tensor_reduce(r_a, rest, AX.X, ALU.max))
            link(dve.tensor_tensor(pick0, rank_all, over_experts(r_a), ALU.is_equal))
            link(dve.scalar_tensor_tensor(rest, pick0, MASKED, logit, ALU.mult, ALU.add))
            link(dve.tensor_reduce(r_a, rest, AX.X, ALU.max))
            link(dve.tensor_tensor(pick1, rest, over_experts(r_a), ALU.is_equal))
            link(dve.tensor_tensor(diff, r_a, top0, ALU.subtract))
            assert done == 3 * T + 1 + 8 + 10
            link(dve.tensor_tensor(pick1, pick1, rank_all, ALU.mult))
            link(dve.tensor_reduce(r_a, pick1, AX.X, ALU.max))
            link(dve.tensor_tensor(pick1, rank_all, over_experts(r_a), ALU.is_equal))
            dve.wait_ge(pre_act, 3 + CT * 4 + 1)
            link(dve.tensor_scalar(p1, ex, 1.0, None, ALU.add))
            link(dve.reciprocal(p0, p1))
            link(dve.tensor_tensor(p1, ex, p0, ALU.mult))
            link(dve.tensor_tensor(pick0, pick0, over_experts(p0), ALU.mult))
            link(dve.tensor_tensor(pick1, pick1, over_experts(p1), ALU.mult))
            link(dve.tensor_tensor(w_tok[:].rearrange("p e t -> p t e"), pick0, pick1, ALU.add))

            with dve.Fori(0, KV) as g:
                wait(dve, acc_done, g, 0)
                dve.tensor_copy(w_tok_g[:], w_tok[:, bass.ds(g * EG, EG), :]).then_inc(wtok_done.sem, 1)
                for step in order:
                    kind, a = step[0], step[1:]
                    if kind == "split_weights":
                        for c in range(CT):
                            qk = w_raw[:, 0:QW + D].rearrange("p (h d) -> p h d", d=D)
                            wait(dve, w_in_sem, g, c + 1)
                            dve.tensor_reduce(head_sum[:], qk, AX.X, ALU.add).then_inc(mean_step.sem, 1)
                            wait(dve, mean_step, g, 3 * c + 1)
                            dve.tensor_scalar(head_mean[:], head_sum[:], 1.0 / D, None, ALU.mult)\
                                .then_inc(mean_step.sem, 1)
                            wait(dve, mean_step, g, 3 * c + 2)
                            dve.tensor_tensor(qk, qk, head_mean[:].unsqueeze(2).to_broadcast([P, HG + 1, D]),
                                              ALU.subtract).then_inc(mean_step.sem, 1)
                            wait(dve, w_hi_done, g, c + 1)
                            dve.tensor_tensor(w_lo[:, c, :], w_raw[:], w_hi[:, c, :].bitcast(F32), ALU.subtract)\
                                .then_inc(w_lo_done.sem, 1)
                    elif kind == "expert_up":
                        m = a[0]
                        if m % 4 == 0:
                            wait(dve, fc_hi_done, g, m // 4 + 1)
                            dve.tensor_tensor(fc_lo[:], fc_raw[:], fc_hi[:].bitcast(F32), ALU.subtract)\
                                .then_inc(fc_lo_done.sem, 1)
                    elif kind == "expert_down":
                        m = a[0]
                        if m == 0:
                            wait(dve, wtok_done, g, 1)
                        for half in range(2):
                            wait_filled(dve, g, "Y", m, half)
                            for k in range(2):
                                tile = (m % 4) * 4 + 2 * half + k
                                n = acc_number["Y", m, half] - 1 + k
                                wait(dve, acc_done, g, acc_before[n])
                                dve.scalar_tensor_tensor(
                                    acc[:, tile, :], bank("Y", m, half)[:, k * C:(k + 1) * C],
                                    w_tok_g[:, m // 4, tile:tile + 1], acc[:, tile, :], ALU.mult, ALU.add)\
                                    .then_inc(acc_done.sem, 1)
                    elif kind == "project":
                        t = a[0]
                        wait(dve, qkv_read, g, 3 * t + 2)
                        dve.tensor_reduce(sumsq[:], squares[:], AX.X, ALU.add).then_inc(sumsq_done.sem, 1)
                        wait(dve, sumsq_done, g, t + 1)
                        dve.tensor_scalar(variance[:], sumsq[:], 1.0 / D, QK_EPS, ALU.mult, ALU.add)\
                            .then_inc(variance_done.sem, 1)
                        wait(dve, tables_done, g, t + 1)
                        wait(dve, rotated_done, g, t)
                        dve.tensor_tensor(t_same[:, 0:HG, :], qk_raw[:, 0:HG, :],
                                          table_same[:, 0:1, :].to_broadcast([P, HG, D]), ALU.mult)
                        dve.tensor_tensor(t_same[:, HG, :], qk_raw[:, HG, :], table_same[:, 1, :], ALU.mult)\
                            .then_inc(same_done.sem, 1)
                        wait(dve, qkv_read, g, 3 * t + 3)
                        dve.tensor_tensor(v_lo[:, t, :], bank("KV", t)[:, D:2 * D], v_hi[:, t, :].bitcast(F32),
                                          ALU.subtract).then_inc(v_lo_done.sem, 1)
                        wait(dve, swap_done, g, t + 1)
                        wait(dve, same_done, g, t + 1)
                        dve.tensor_tensor(t_same[:], t_same[:], t_swap[:], ALU.add).then_inc(both_done.sem, 1)
                        wait(dve, both_done, g, t + 1)
                        wait(dve, rstd_done, g, t + 1)
                        for h in range(HG + 1):
                            ins = dve.scalar_tensor_tensor(rotated[:, h, :], t_same[:, h, :], rstd[:, h:h + 1],
                                                           table_bias[:, h // HG, :], ALU.mult, ALU.add)
                        ins.then_inc(rotated_done.sem, 1)
                    elif kind == "turn_qk":
                        t = a[0]
                        wait(dve, qk_hi_done, g, 2 * t + 1)
                        dve.tensor_tensor(qT_lo[:], bank("QT", t)[:], qT_hi[:].bitcast(F32),
                                          ALU.subtract).then_inc(qk_lo_done.sem, 1)
                        wait(dve, qk_hi_done, g, 2 * t + 2)
                        cols = slice(t * P, (t + 1) * P)
                        dve.tensor_tensor(kT_lo[:, cols], bank("KT", t)[:, 0:P], kT_hi[:, cols].bitcast(F32),
                                          ALU.subtract).then_inc(qk_lo_done.sem, 1)
                    elif kind == "scores":
                        t, h, c = a
                        u, w, n = (2 * t + h // 2) % 2, chunks_of(t)[c], len(chunks_of(t))
                        wait_filled(dve, g, "S", t, h, c)
                        nm = neg_max[:, u, h % 2:h % 2 + 1]
                        if n == 1:
                            dve.tensor_reduce(nm, bank("S", t, h, c)[:, 0:w], AX.X, ALU.max, negate=True)\
                                .then_inc(neg_max_done.sem, 1)
                            dve.sem_inc(chunk_max_done.sem, 1)
                        else:
                            dve.tensor_reduce(neg_chunk_max[:, u, h % 2, c:c + 1], bank("S", t, h, c)[:, 0:w],
                                              AX.X, ALU.max, negate=True).then_inc(chunk_max_done.sem, 1)
                            if c == n - 1:
                                wait(dve, chunk_max_done, g, number[step])
                                dve.tensor_reduce(nm, neg_chunk_max[:, u, h % 2, 0:n], AX.X, ALU.min)\
                                    .then_inc(neg_max_done.sem, 1)
                    elif kind == "turn_probs":
                        t, p, i = a
                        n = number[step]
                        w = 256 * min(2, t + 1 - 2 * i)
                        wait(dve, pt_hi_done, g, n)
                        dve.tensor_tensor(pT_lo[:, n % PT_RING, 0:w], pt_bank[n % 2][:, 0:w],
                                          pT_hi[:, n % PT_RING, 0:w].bitcast(F32), ALU.subtract)\
                            .then_inc(pt_lo_done.sem, 1)
                    elif kind == "turn_gate":
                        t = a[0]
                        n = len(chunks_of(t))
                        wait(dve, exp_done, g, number["exp", t, HG - 1, n - 1])
                        dve.tensor_reduce(row_sum[:], chunk_sum[:, t % 2, :, 0:n], AX.X, ALU.add)\
                            .then_inc(sum_step.sem, 1)
                        wait(dve, sum_step, g, 2 * t + 1)
                        dve.tensor_scalar(twice_sum[:], row_sum[:], 2.0, None, ALU.mult).then_inc(sum_step.sem, 1)
                        wait(dve, sum_step, g, 2 * t + 2)
                        wait(dve, gated, g, t)
                        dve.reciprocal(half_inv[:], twice_sum[:]).then_inc(inv_done.sem, 1)
                    elif kind == "project_out":
                        t = a[0]
                        wait_filled(dve, g, "GT", t)
                        wait(dve, o_copied, g, 2 * t + 2)
                        wait(dve, filled, g, number["fill", ("OUT", t - 1)] if t else 0)
                        dve.tensor_tensor(ogT[:], bank("GT", t)[:], oT[:], ALU.mult)\
                            .then_inc(og_done.sem, 1)
                        wait_filled(dve, g, "OUT", t)
                        n = acc_number["OUT", t]
                        wait(dve, acc_done, g, acc_before[n])
                        dve.tensor_tensor(acc[:, t, :], bank("OUT", t)[:, 0:C], acc[:, t, :], ALU.add)\
                            .then_inc(acc_done.sem, 1)

        @block.tensor
        def _(pe):
            for s in (filled, pt_filled, pv_done):
                pe.sem_inc(s.sem, 1)
            pe.wait_ge(consts_in, 48)
            for i in range(CT * 4):
                if i >= 4:
                    pe.wait_ge(pre_dve, 3 * T + 1 + i - 3)
                for k in range(4):
                    t = 4 * (i // 2) + k
                    pe.wait_ge(pre_dve, 2 * T + t + 1)
                    ins = pe.transpose(banks[i % 4][:, k * P:(k + 1) * P], xn[:, t, (i % 2) * P:(i % 2 + 1) * P],
                                       ident_f[:])
                ins.then_inc(pre_pe, 1)
            pe.wait_ge(pre_dve, 3 * T + 1 + CT * 4)
            for t in range(T):
                rows = slice(t * P, (t + 1) * P)
                todo = [(xs, ws, c) for c in range(CT) for xs, ws in
                        ((xT_hi, wr_hi), (xT_hi, wr_lo), (xT_lo, wr_hi))]
                for n, (xs, ws, c) in enumerate(todo):
                    ins = pe.matmul(banks[4][:, t * E:(t + 1) * E], xs[:, c, rows], ws[:, c, :],
                                    start=(n == 0), stop=(n == len(todo) - 1))
            ins.then_inc(pre_pe, 1)
            pe.wait_ge(pre_dve, 3 * T + 1 + CT * 4 + 1)
            pe.wait_ge(pre_act, 3 + CT * 4)

            def three(out_ap, stationary, moving, start=True, stop=True):
                n, last = len(stationary), 3 * len(stationary)
                done = 0
                for (s_hi, s_lo), (m_hi, m_lo) in zip(stationary, moving):
                    for s, m in ((s_hi, m_hi), (s_hi, m_lo), (s_lo, m_hi)):
                        done += 1
                        ins = pe.matmul(out_ap, s, m, start=(start and done == 1), stop=(stop and done == last))
                return ins

            with pe.Fori(0, KV) as g:
                for step in order:
                    kind, a = step[0], step[1:]
                    if kind == "expert_up":
                        m = a[0]
                        e, cols = m // 4, slice((m % 4) * CHUNK, (m % 4 + 1) * CHUNK)
                        if m % 4 == 0:
                            wait(pe, fc_lo_done, g, e + 1)
                        for d in range(2):
                            ds = slice(d * P, (d + 1) * P)
                            wait_bank_free(pe, g, "H", m, d)
                            three(bank("H", m, d)[:],
                                  [(fc_hi[:, c, ds], fc_lo[:, c, ds]) for c in range(CT)],
                                  [(xT_hi[:, c, cols], xT_lo[:, c, cols]) for c in range(CT)])\
                                .then_inc(filled.sem, 1)
                    elif kind == "expert_down":
                        m = a[0]
                        if m % 4 == 0:
                            wait(pe, pj_in, g, m // 4 + 1)
                        wait(pe, hidden_done, g, m + 1)
                        for half in range(2):
                            wait_bank_free(pe, g, "Y", m, half)
                            for k in range(2):
                                for d in range(2):
                                    cols = slice((2 * half + k) * P, (2 * half + k + 1) * P)
                                    ins = pe.matmul(bank("Y", m, half)[:, k * C:(k + 1) * C], hidden[:, d, cols],
                                                    pj_sb[:, d, :], start=(d == 0), stop=(d == 1))
                            ins.then_inc(filled.sem, 1)
                    elif kind == "project":
                        t = a[0]
                        rows = slice(t * P, (t + 1) * P)
                        if t == 0:
                            wait(pe, w_lo_done, g, CT)
                        for part, cols in (("Q", slice(0, QW)), ("KV", slice(QW, QW + 2 * D)),
                                           ("G", slice(QW + 2 * D, WCOLS))):
                            wait_bank_free(pe, g, part, t)
                            three(bank(part, t)[:, 0:cols.stop - cols.start],
                                  [(xT_hi[:, c, rows], xT_lo[:, c, rows]) for c in range(CT)],
                                  [(w_hi[:, c, cols], w_lo[:, c, cols]) for c in range(CT)])\
                                .then_inc(filled.sem, 1)
                    elif kind == "turn_qk":
                        t = a[0]
                        wait(pe, rotated_done, g, t + 1)
                        wait_bank_free(pe, g, "QT", t)
                        for h in range(HG):
                            ins = pe.transpose(bank("QT", t)[:, h * P:(h + 1) * P], rotated[:, h, :], ident_f[:])
                        ins.then_inc(filled.sem, 1)
                        wait_bank_free(pe, g, "KT", t)
                        pe.transpose(bank("KT", t)[:, 0:P], rotated[:, HG, :], ident_f[:]).then_inc(filled.sem, 1)
                    elif kind == "scores":
                        t, h, c = a
                        w = chunks_of(t)[c]
                        if h == 0 and c == 0:
                            wait(pe, qk_lo_done, g, 2 * t + 2)
                        heads, keys = slice(h * P, (h + 1) * P), slice(c * CHUNK, c * CHUNK + w)
                        wait_bank_free(pe, g, "S", t, h, c)
                        diagonal = c == len(chunks_of(t)) - 1
                        ins = three(bank("S", t, h, c)[:, 0:w],
                                    [(qT_hi[:, heads], qT_lo[:, heads])],
                                    [(kT_hi[:, keys], kT_lo[:, keys])], stop=not diagonal)
                        if diagonal:
                            ins = pe.matmul(bank("S", t, h, c)[:, w - P:w], ident_b[:], mask_b[:],
                                            start=False, stop=True)
                        ins.then_inc(filled.sem, 1)
                    elif kind == "turn_probs":
                        t, p, i = a
                        n = number[step]
                        wait(pe, exp_done, g, max(number["exp", t, 2 * p + hh, min(2 * i + 1, t) // 4]
                                                  for hh in range(2)))
                        wait(pe, pt_lo_done, g, n - 2)
                        for jj in range(min(2, t + 1 - 2 * i)):
                            for hh in range(2):
                                j = 2 * i + jj
                                ins = pe.transpose(pt_bank[n % 2][:, (2 * jj + hh) * P:(2 * jj + hh + 1) * P],
                                                   probs[:, (2 * t + p) % 2, hh, j * P:(j + 1) * P], ident_f[:])
                        ins.then_inc(pt_filled.sem, 1)
                    elif kind == "pv":
                        t, p, i = a
                        n = number[step]
                        wait(pe, pt_lo_done, g, n)
                        if i == 0:
                            wait(pe, o_copied, g, 2 * t + p)
                            wait(pe, v_lo_done, g, t + 1)
                        for jj in range(min(2, t + 1 - 2 * i)):
                            j, cols = 2 * i + jj, slice(2 * jj * P, 2 * (jj + 1) * P)
                            ins = three(o_bank[:, 256 * p:256 * p + 256], [(v_hi[:, j, :], v_lo[:, j, :])],
                                        [(pT_hi[:, n % PT_RING, cols], pT_lo[:, n % PT_RING, cols])],
                                        start=(j == 0), stop=(j == t))
                        ins.then_inc(pv_done.sem, 1)
                    elif kind == "turn_gate":
                        t = a[0]
                        wait(pe, gated, g, t + 1)
                        wait_bank_free(pe, g, "GT", t)
                        for h in range(HG):
                            ins = pe.transpose(bank("GT", t)[:, h * P:(h + 1) * P],
                                               gate[:, t % 2, h * D:(h + 1) * D], ident_f[:])
                        ins.then_inc(filled.sem, 1)
                    elif kind == "project_out":
                        t = a[0]
                        wait(pe, og_done, g, t + 1)
                        if t == 0:
                            wait(pe, wo_in, g, 1)
                        wait_bank_free(pe, g, "OUT", t)
                        for h in range(HG):
                            ins = pe.matmul(bank("OUT", t)[:, 0:C], ogT[:, h * P:(h + 1) * P], wo_sb[:, h, :],
                                            start=(h == 0), stop=(h == HG - 1))
                        ins.then_inc(filled.sem, 1)


def kernel(L0_attn_x, L0_attn_w_qkv, L0_attn_w_o, L0_attn_q_norm_w, L0_attn_q_norm_b, L0_attn_k_norm_w,
           L0_attn_k_norm_b, L0_ffn_w_router, L0_ffn_w_fc, L0_ffn_w_proj):
    import concourse.bacc as bacc
    from concourse.bass_utils import run_bass_kernel_spmd

    pairs = np.concatenate([np.arange(0, D, 2), np.arange(1, D, 2)])
    w = np.asarray(L0_attn_w_qkv)
    wq = w[0:H * D].reshape(KV, HG, D, C)[:, :, pairs].reshape(KV, HG * D, C)
    wg = w[H * D:2 * H * D].reshape(KV, HG * D, C)
    wk = w[2 * H * D:2 * H * D + KV * D].reshape(KV, D, C)[:, pairs]
    wv = w[2 * H * D + KV * D:].reshape(KV, D, C)
    w_in = np.concatenate([wq, wk, wv, wg], axis=1).transpose(0, 2, 1).reshape(KV, CT, P, WCOLS)
    inv = np.float32(1.0) / np.power(np.float32(ROPE_BASE), np.arange(0, D, 2, dtype=np.float32) / np.float32(D))
    angles = np.outer(np.arange(S, dtype=np.float32), inv.astype(np.float32)).astype(np.float32)
    arrays = {
        "x": np.asarray(L0_attn_x).reshape(S, C),
        "w_in": w_in,
        "w_o": np.asarray(L0_attn_w_o).T.reshape(KV, HG * D, C),
        "q_w": np.asarray(L0_attn_q_norm_w)[pairs],
        "q_b": np.asarray(L0_attn_q_norm_b)[pairs],
        "k_w": np.asarray(L0_attn_k_norm_w)[pairs],
        "k_b": np.asarray(L0_attn_k_norm_b)[pairs],
        "w_router": np.asarray(L0_ffn_w_router),
        "w_fc": np.asarray(L0_ffn_w_fc).reshape(KV, EG, C, C),
        "w_proj": np.asarray(L0_ffn_w_proj).reshape(KV, EG, C, C),
        "cos": np.cos(angles),
        "sin": np.sin(angles),
        "ident": np.eye(P, dtype=np.float32),
        "mask": np.triu(np.full((P, P), MASKED, np.float32), 1),
    }
    arrays = {n: np.ascontiguousarray(a) for n, a in arrays.items()}
    nc = bacc.Bacc("TRN2", target_bir_lowering=False, num_devices=1)
    args = [nc.dram_tensor(f"in_{n}", a.shape, mybir.dt.from_np(a.dtype), kind="ExternalInput").ap()
            for n, a in arrays.items()]
    args.append(nc.dram_tensor("out_0", (S, C), F32, kind="ExternalOutput").ap())
    build(nc, *args)
    r = run_bass_kernel_spmd(nc, [{f"in_{n}": a for n, a in arrays.items()}], core_ids=[0])
    return r.results[0]["out_0"].reshape(1, S, C)
```

```python
from contextlib import ExitStack

import numpy as np

import concourse.bass as bass
from concourse import mybir

F32 = mybir.dt.float32
F32R = mybir.dt.float32r
BF16 = mybir.dt.bfloat16
ALU = mybir.AluOpType
ACT = mybir.ActivationFunctionType
AX = mybir.AxisListType

P = 128
S = 2048
C = 256
D = 128
H = 16
KV = 4
HG = H // KV
E = 8
T = S // P
CT = C // P
CHUNK = 512
ROPE_BASE = 1000000.0
LN_EPS = 1e-5
QK_EPS = 1e-6
MASKED = -3.0e38
NBANK = 5
PT_RING = 3
QW = HG * D
WCOLS = 2 * QW + 2 * D
EG = E // KV
JOBS = EG * (S // CHUNK)
SCORE_BANKS = {1: (0, 1, 2), 2: (0, 1, 2), 3: (0, 1, 2, 3), 4: (0, 1, 2, 3)}
OTHER_BANKS = {1: (3, 4), 2: (3, 4), 3: (4,), 4: (4,)}
FILLS = ("Q", "KV", "G", "QT", "KT", "GT", "OUT", "H", "Y", "scores")
HANDOVER = {"pe": 0.21, "act": 0.14, "dve": 0.12, "pool": 0.2}
DUE = {"start": 14.9, "per_step": 1.17, "per_chunk": 1.29, "per_unit": -3.9, "rope": -12.6, "v_lo": -55.0,
       "rope_b": -20.2, "turn": -28.6, "gate": 5.9, "inv": 6.6, "scale": 24.8, "turn_gate": 2.4, "og": 3.2,
       "out": 12.2, "out_add": 20.8, "scores": -14.2, "max": 38.5, "exp": 4.7, "prob_step": 1.12, "pv": 7.9,
       "p_hi": 3.7, "p_lo": 5.5, "expert": 0.0, "expert_step": 1.0, "evict": -100.0, "evict_step": 12.0,
       "first_half": 0.0, "window": 0.0}


def freed_by_step(step):
    kind, a = step[0], step[1:]
    return ({"Q": "q_take", "KV": "v_lo", "G": "tanh", "QT": "q_lo", "KT": "k_lo", "GT": "og", "OUT": "out_add",
             "scores": "exp", "H": "relu", "Y": "y_add"}[kind], *a)


class Steps:

    def __init__(self, sem, per, unit=1):
        self.sem, self.per, self.unit = sem, per, unit

    def after(self, g, n):
        return g * (self.per * self.unit) + (1 + max(n, 0) * self.unit)


def chunks_of(t):
    width = (t + 1) * P
    return [min(CHUNK, width - c) for c in range(0, width, CHUNK)]


def due_times():
    begin, now = {}, DUE["start"]
    for t in range(T):
        for p in range(HG // 2):
            begin[t, p] = now
            now += DUE["per_step"] * ((t + 2) // 2) + DUE["per_chunk"] * len(chunks_of(t)) + DUE["per_unit"]
    begin[T, 0] = begin[T, 1] = now
    return begin


def group_steps():
    begin = due_times()
    steps = []

    def add(queue, step, cost, needs, due):
        steps.append((queue, step, cost, [n for n in needs if n is not None], due))

    def old(tile, *step):
        return step if tile >= 0 else None

    n = 0
    prob_steps = [(t, p, i) for t in range(T) for p in range(HG // 2) for i in range((t + 2) // 2)]
    for e in range(EG):
        before = ("H", 4 * e - 1, 1) if e else None
        add("act fc", ("fc_hi", e), 0.5, [before], 60 * e)
        add("dve fc", ("fc_lo", e), 0.65, [("fc_hi", e)], 60 * e)
    for c in range(CT):
        add("dve w", ("centre", c), 2.2, [("w_low", c - 1)] if c else [], -9)
        add("act w", ("w_high", c), 1.1, [("centre", c)], -9)
        add("dve w", ("w_low", c), 1.4, [("w_high", c)], -9)
    for m in range(JOBS):
        for d in range(2):
            add("pe H", ("H", m, d), 1.3, [("fc_lo", m // 4), ("Y", m - 1, 1) if m else None], DUE["expert"] + DUE["expert_step"] * m)
            add("act H", ("relu", m, d), 0.5, [("H", m, d), ("Y", m - 1, 1) if m else None], DUE["evict"] + DUE["evict_step"] * m)
        add("act H", ("square", m), 0.95, [("relu", m, 1)], DUE["evict"] + DUE["evict_step"] * m)
        for half in range(2):
            add("pe Y", ("Y", m, half), 1.75, [("square", m)], DUE["expert"] + DUE["expert_step"] * m - 0.5)
            add("dve Y", ("y_add", m, half), 0.8, [("Y", m, half)], DUE["evict"] + DUE["evict_step"] * m - 10)
    add("pool", ("tables", 0), 3.6, [], 0)
    for t in range(T):
        b0, b1, b2 = begin[t, 0], begin[t, 1], begin[t + 1, 0]
        add("pe QKV", ("Q", t), 1.3, [("w_low", 1), old(t - 1, "KT", t - 1)], b0 + DUE["rope"])
        add("pe QKV", ("KV", t), 0.65, [("w_low", 1)], b0 + DUE["rope"])
        add("pe G", ("G", t), 1.3, [("w_low", 1), old(t - 2, "GT", t - 2)], b1 + DUE["gate"])
        add("act QKV", ("q_take", t), 0.95, [("Q", t)] + [old(t - 1, x, t - 1) for x in ("same", "swap", "KT")],
            b0 + DUE["rope"])
        add("act QKV", ("kv_take", t), 0.5, [("KV", t)], b0 + DUE["rope"])
        add("dve rope", ("sumsq", t), 0.95, [("kv_take", t)], b0 + DUE["rope"])
        add("dve rope", ("same", t), 0.85, [("kv_take", t), ("tables", t), old(t - 1, "rope_b", t - 1)], b0 + DUE["rope"])
        add("dve v", ("v_lo", t), 0.2, [("kv_take", t)], b0 + DUE["v_lo"])
        add("pool", ("swap", t), 2.0, [("kv_take", t), old(t - 1, "rope_b", t - 1)], 0)
        add("pool", ("rstd", t), 1.2, [("sumsq", t)], 0)
        add("dve rope", ("rope_b", t), 2.2, [("swap", t), ("rstd", t)], b0 + DUE["rope_b"])
        if t + 1 < T:
            add("pool", ("tables", t + 1), 3.6, [("rope_b", t), ("same", t)], 0)
        last = len(chunks_of(t - 1)) - 1 if t else 0
        add("pe turn", ("QT", t), 0.43, [("rope_b", t), old(t - 1, "scores", t - 1, HG - 1, last)], b0 + DUE["turn"])
        add("pe turn", ("KT", t), 0.11, [("rope_b", t)], b0 + DUE["turn"])
        add("act turn", ("q_hi", t), 0.48, [("QT", t)], b0 + DUE["turn"])
        add("act turn", ("k_hi", t), 0.16, [("KT", t)], b0 + DUE["turn"])
        add("dve turn", ("q_lo", t), 0.6, [("q_hi", t)], b0 + DUE["turn"])
        add("dve turn", ("k_lo", t), 0.2, [("k_hi", t)], b0 + DUE["turn"])
        add("act gate", ("tanh", t), 0.48, [("G", t), old(t - 2, "GT", t - 2)], b1 + DUE["gate"])
        add("dve gate", ("inv", t), 0.5, [("exp", t, HG - 1, len(chunks_of(t)) - 1),
                                          old(t - 1, "gate_scale", t - 1)], b2 + DUE["inv"])
        add("act gate", ("gate_scale", t), 1.55, [("inv", t), ("tanh", t)], b2 + DUE["scale"])
        add("pe GT", ("GT", t), 0.43, [("gate_scale", t), ("o_take", t, 1), old(t - 1, "OUT", t - 1)], b2 + DUE["turn_gate"])
        add("dve out", ("og", t), 0.6, [("GT", t), ("o_take", t, 1), old(t - 1, "OUT", t - 1)], b2 + DUE["og"])
        add("pe OUT", ("OUT", t), 1.75, [("og", t)], b2 + DUE["out"])
        add("dve out", ("out_add", t), 0.33, [("OUT", t)], b2 + DUE["out_add"])
        for h in range(HG):
            p, hh = h // 2, h % 2
            start = begin[t, 0] if p == 0 else begin[t, 1]
            prev = begin[(t, 0) if p else (t - 1, 1)] if (t or p) else start - 6
            at = start - (start - prev) * (DUE["first_half"] if hh == 0 else 0.0)
            lag_exp = ("exp", t - 1, h, len(chunks_of(t - 1)) - 1) if t else None
            for c, w in enumerate(chunks_of(t)):
                add("pe S", ("scores", t, h, c), 3 * w / 2400 + 0.05, [("k_lo", t)], at + DUE["scores"])
                add("dve S", ("max", t, h, c), 0.07 + w / 960 + (0.2 if 0 < c == len(chunks_of(t)) - 1 else 0.0), [("scores", t, h, c), lag_exp], at + DUE["max"])
            for c, w in enumerate(chunks_of(t)):
                free = ("turn_probs", t - 1, p, (t + 1) // 2 - 1) if t else None
                add("act S", ("exp", t, h, c), 0.24 + w / 1200, [("max", t, h, len(chunks_of(t)) - 1), free,
                                                                 old(t - 2, "inv", t - 2)], at + DUE["exp"])
        for p in range(HG // 2):
            last = (t + 2) // 2 - 1
            for i in range(last + 1):
                two = min(2, t + 1 - 2 * i)
                d = begin[t, p] + DUE["prob_step"] * i
                old_p = [prob_steps[n - k] if n >= k else None for k in (2, 3)]
                exps = [("exp", t, 2 * p + hh, min(2 * i + 1, t) // 4) for hh in range(2)]
                add("pe PT", ("turn_probs", t, p, i), 0.215 * two,
                    exps + [("p_lo", *old_p[0]) if old_p[0] else None], d)
                add("act PT", ("p_hi", t, p, i), 0.05 + 0.215 * two,
                    [("turn_probs", t, p, i), ("pv", *old_p[1]) if old_p[1] else None], d + DUE["p_hi"])
                add("dve PT", ("p_lo", t, p, i), 0.07 + 0.265 * two, [("p_hi", t, p, i)], d + DUE["p_lo"])
                prev_take = (("o_take", t, p - 1) if p else old(t - 1, "o_take", t - 1, 1)) if i == 0 else None
                add("pe PV", ("pv", t, p, i), 0.325 * two, [("p_lo", t, p, i), ("v_lo", t), prev_take], d + DUE["pv"])
                n += 1
            add("act O", ("o_take", t, p), 0.27, [("pv", t, p, last), old(t - 1, "og", t - 1)], begin[t, p] + DUE["prob_step"] * last)
    return steps


def plan_group():
    queues, cost, needs, due, on = {}, {}, {}, {}, {}
    for queue, step, c, need, when in group_steps():
        queues.setdefault(queue, []).append(step)
        cost[step], needs[step], due[step], on[step] = c, need, when, queue.split()[0]
    engines = {"pe": [], "act": [], "dve": [], "pool": []}
    clock = dict.fromkeys(engines, 0.0)
    done, bank_of, prior = {}, {}, {}
    held = [None] * NBANK
    width = [1]

    def bank_for(step):
        if step[0] == "scores":
            allowed = SCORE_BANKS[len(chunks_of(step[1]))]
        else:
            allowed = OTHER_BANKS[width[0]]
        free = []
        for b in allowed:
            if held[b] is None:
                free.append((0.0, b))
            elif freed_by_step(held[b]) in done:
                free.append((done[freed_by_step(held[b])], b))
        return min(free) if free else None

    left = sum(len(q) for q in queues.values())
    while left:
        best = None
        for queue, waiting in queues.items():
            if not waiting:
                continue
            step, engine = waiting[0], queue.split()[0]
            if any(x not in done for x in needs[step]):
                continue
            start = max([done[x] + (HANDOVER[on[x]] if on[x] != engine else 0.0) for x in needs[step]] + [0.0])
            if step[0] in FILLS:
                free = bank_for(step)
                if free is None:
                    continue
                start = max(start, free[0] + 0.1)
            start = max(start, clock[engine])
            now = start <= clock[engine] + DUE["window"]
            key = (start if not now else clock[engine], due[step])
            if best is None or key < best[0]:
                best = (key, queue, step, engine, start)
        _, queue, step, engine, start = best
        queues[queue].pop(0)
        left -= 1
        if step[0] in FILLS:
            b = bank_for(step)[1]
            bank_of[step], prior[step], held[b] = b, held[b], step
            if step[0] == "scores":
                width[0] = len(chunks_of(step[1]))
        clock[engine] = done[step] = start + cost[step]
        engines[engine].append(step)
    return engines, bank_of, prior


def build(nc, x, w_in, w_o, q_w, q_b, k_w, k_b, w_router, w_fc, w_proj, cos, sin, ident, mask, out):
    order, bank_of, prior = plan_group()
    number, total = {}, {}
    for engine in order.values():
        for step in engine:
            total[step[0]] = total.get(step[0], 0) + 1
            number[step] = total[step[0]]
    for n, step in enumerate(bank_of):
        number["fill", step] = n + 1
    n_many = sum(len(chunks_of(t)) for t in range(T) if len(chunks_of(t)) > 1) * HG

    with ExitStack() as ctx:
        def sb(name, shape, dt=F32):
            return ctx.enter_context(nc.sbuf_tensor(name, shape, dt))

        def sem(name):
            return ctx.enter_context(nc.semaphore(name))

        acc = sb("acc", [P, T, C])
        xT_hi = sb("xT_hi", [P, CT, S], F32R)
        xT_lo = sb("xT_lo", [P, CT, S], F32R)
        w_raw = sb("w_raw", [P, WCOLS])
        w_hi = sb("w_hi", [P, CT, WCOLS], F32R)
        w_lo = sb("w_lo", [P, CT, WCOLS], F32R)
        kT_hi = sb("kT_hi", [P, S], F32R)
        kT_lo = sb("kT_lo", [P, S], F32R)
        v_hi = sb("v_hi", [P, T, D], F32R)
        v_lo = sb("v_lo", [P, T, D], F32R)
        cos_sb = sb("cos_sb", [P, T, D // 2])
        sin_sb = sb("sin_sb", [P, T, D // 2])
        probs = sb("probs", [P, 2, 2, S])
        wo_sb = sb("wo_sb", [P, HG, C])
        qT_hi = sb("qT_hi", [P, QW], F32R)
        qT_lo = sb("qT_lo", [P, QW], F32R)
        pT_hi = sb("pT_hi", [P, PT_RING, CHUNK], F32R)
        pT_lo = sb("pT_lo", [P, PT_RING, CHUNK], F32R)
        qk_raw = sb("qk_raw", [P, HG + 1, D])
        squares = sb("squares", [P, HG + 1, D])
        rotated = squares
        t_same = sb("t_same", [P, HG + 1, D])
        t_swap = sb("t_swap", [P, HG + 1, D])
        table_same = sb("table_same", [P, 2, D])
        table_swap = sb("table_swap", [P, 2, D])
        table_bias = sb("table_bias", [P, 2, D])
        bias_part = t_swap[:, 0:2, :]
        gate = sb("gate", [P, 2, QW])
        oT = sb("oT", [P, QW])
        ogT = sb("ogT", [P, QW])
        fc_raw = sb("fc_raw", [P, CT, C])
        fc_hi = sb("fc_hi", [P, CT, C], F32R)
        fc_lo = sb("fc_lo", [P, CT, C], F32R)
        pj_sb = sb("pj_sb", [P, CT, C])
        hidden = sb("hidden", [P, 2, CHUNK])
        ident_f = sb("ident_f", [P, P])
        ident_b = sb("ident_b", [P, P], BF16)
        mask_b = sb("mask_b", [P, P], BF16)
        ln_w = sb("ln_w", [P, 2, D])
        ln_b = sb("ln_b", [P, 2, D])
        ln_ws = sb("ln_ws", [P, 2, D])
        ln_bs = sb("ln_bs", [P, 2, D])
        head_sum = sb("head_sum", [P, HG + 1])
        head_mean = sb("head_mean", [P, HG + 1])
        sumsq = sb("sumsq", [P, HG + 1])
        variance = sb("variance", [P, HG + 1])
        rstd = sb("rstd", [P, HG + 1])
        minus_half = sb("minus_half", [P, T])
        neg_chunk_max = sb("neg_chunk_max", [P, 2, 2, 4])
        neg_max = sb("neg_max", [P, 2, 2])
        chunk_sum = sb("chunk_sum", [P, 2, HG, 4])
        row_sum = sb("row_sum", [P, HG])
        twice_sum = sb("twice_sum", [P, HG])
        half_inv = sb("half_inv", [P, HG])
        wr_hi = sb("wr_hi", [P, CT, E], F32R)
        wr_lo = sb("wr_lo", [P, CT, E], F32R)
        w_tok = sb("w_tok", [P, E, T])
        w_tok_g = sb("w_tok_g", [P, EG, T])
        xn = probs[:, 0, :, :].rearrange("p a (t c) -> p (a t) c", c=C)
        rt = [probs[:, 1, 0, i * T * E:(i + 1) * T * E].rearrange("p (t e) -> p t e", e=E) for i in range(4)]
        x_stats = probs[:, 1, 1, 0:T * 6].rearrange("p (t s) -> p t s", s=6)
        x_mv = probs[:, 1, 1, 128:128 + 2 * T].rearrange("p (t s) -> p t s", s=2)
        x_var = probs[:, 1, 1, 192:192 + T]
        x_rstd = probs[:, 1, 1, 224:224 + T]
        rank = probs[:, 1, 1, 256:256 + E]
        wr_raw = probs[:, 1, 1, 288:288 + CT * E].rearrange("p (a e) -> p a e", e=E)
        rs = [probs[:, 1, 1, 320 + 32 * i:320 + 32 * i + T] for i in range(6)]
        mask_f = hidden[:, 0, 0:P]

        banks = [ctx.enter_context(nc.psum_tensor(f"bank{b}", [P, CHUNK], F32)) for b in range(NBANK)]
        pt_bank = [ctx.enter_context(nc.psum_tensor(f"pt_bank{b}", [P, CHUNK], F32)) for b in range(2)]
        o_bank = ctx.enter_context(nc.psum_tensor("o_bank", [P, CHUNK], F32))

        def bank(*step):
            return banks[bank_of[step]]

        x_in, tables_in, consts_in = sem("x_in"), sem("tables_in"), sem("consts_in")
        pre_dve, pre_pool, pre_act, pre_pe = sem("pre_dve"), sem("pre_pool"), sem("pre_act"), sem("pre_pe")
        stored = sem("stored")

        filled = Steps(sem("filled"), len(bank_of))
        pt_filled = Steps(sem("pt_filled"), total["turn_probs"])
        pv_done = Steps(sem("pv_done"), total["pv"])
        w_in_sem = Steps(sem("w_loaded"), CT, 16)
        wo_in = Steps(sem("wo_loaded"), 1, 16)
        fc_in = Steps(sem("fc_loaded"), EG, 16)
        pj_in = Steps(sem("pj_loaded"), EG, 16)
        mean_step = Steps(sem("mean_step"), 3 * CT)
        w_hi_done = Steps(sem("w_hi_done"), CT)
        w_lo_done = Steps(sem("w_lo_done"), CT)
        fc_hi_done = Steps(sem("fc_hi_done"), EG)
        fc_lo_done = Steps(sem("fc_lo_done"), EG)
        wtok_done = Steps(sem("wtok_done"), 1)
        qkv_read = Steps(sem("qkv_read"), 3 * T)
        v_lo_done = Steps(sem("v_lo_done"), T)
        gate_done = Steps(sem("gate_done"), T)
        sumsq_done = Steps(sem("sumsq_done"), T)
        variance_done = Steps(sem("variance_done"), T)
        rstd_done = Steps(sem("rstd_done"), T)
        bias_parts = Steps(sem("bias_parts"), T)
        tables_done = Steps(sem("tables_done"), T)
        same_done = Steps(sem("same_done"), T)
        swap_done = Steps(sem("swap_done"), T)
        both_done = Steps(sem("both_done"), T)
        rotated_done = Steps(sem("rotated_done"), T)
        qk_hi_done = Steps(sem("qk_hi_done"), 2 * T)
        qk_lo_done = Steps(sem("qk_lo_done"), 2 * T)
        n_chunks = total["scores"]
        chunk_max_done = Steps(sem("chunk_max_done"), n_many)
        neg_max_done = Steps(sem("neg_max_done"), T * HG)
        exp_done = Steps(sem("exp_done"), n_chunks)
        pt_hi_done = Steps(sem("pt_hi_done"), total["turn_probs"])
        pt_lo_done = Steps(sem("pt_lo_done"), total["turn_probs"])
        o_copied = Steps(sem("o_copied"), T * HG // 2)
        sum_step = Steps(sem("sum_step"), 2 * T)
        inv_done = Steps(sem("inv_done"), T)
        gated = Steps(sem("gated"), T)
        og_done = Steps(sem("og_done"), T)
        relu_done = Steps(sem("relu_done"), 2 * JOBS)
        hidden_done = Steps(sem("hidden_done"), JOBS)
        acc_done = Steps(sem("acc_done"), T + 4 * JOBS)

        freed_by = {
            "Q": lambda t: (qkv_read, 3 * t + 1),
            "KV": lambda t: (v_lo_done, t + 1),
            "G": lambda t: (gate_done, t + 1),
            "QT": lambda t: (qk_lo_done, 2 * t + 1),
            "KT": lambda t: (qk_lo_done, 2 * t + 2),
            "GT": lambda t: (og_done, t + 1),
            "OUT": lambda t: (acc_done, acc_number["out_add", t]),
            "scores": lambda t, h, c: (exp_done, number["exp", t, h, c]),
            "H": lambda m, d: (relu_done, 2 * m + d + 1),
            "Y": lambda m, half: (acc_done, acc_number["y_add", m, half]),
        }
        acc_number, acc_before, last_add, adds = {}, {}, {}, 0
        for step in order["dve"]:
            if step[0] == "out_add":
                tiles = [step[1]]
            elif step[0] == "y_add":
                tiles = [(step[1] % 4) * 4 + 2 * step[2] + k for k in range(2)]
            else:
                continue
            for tile in tiles:
                adds += 1
                acc_before[adds] = last_add.get(tile, 0)
                last_add[tile] = adds
            acc_number[step] = adds
        last_fill = [None] * NBANK
        for step, b in bank_of.items():
            last_fill[b] = step

        def wait(eng, steps, g, n):
            eng.wait_ge(steps.sem, steps.after(g, n))

        def wait_bank_free(eng, g, *step):
            before = prior[step]
            if before is None:
                s, _ = freed_by[last_fill[bank_of[step]][0]](*last_fill[bank_of[step]][1:])
                wait(eng, s, g, 0)
            else:
                s, n = freed_by[before[0]](*before[1:])
                wait(eng, s, g, n)

        def wait_filled(eng, g, *step):
            wait(eng, filled, g, number["fill", step])

        block = ctx.enter_context(nc.Block())

        @block.sync
        def _(sp):
            x_tiles = x.rearrange("(t p) c -> p t c", p=P)
            for q in range(4):
                sp.dma_start(acc[:, 4 * q:4 * q + 4, :], x_tiles[:, 4 * q:4 * q + 4, :]).then_inc(x_in, 16)
            sp.dma_start(ident_f[:], ident).then_inc(consts_in, 16)
            sp.dma_start(mask_f, mask).then_inc(consts_in, 16)
            sp.dma_start(wr_raw, w_router.rearrange("(a p) e -> p a e", p=P)).then_inc(consts_in, 16)
            for i, v in enumerate((q_w, k_w)):
                sp.dma_start(ln_w[:, i, :], v.partition_broadcast(P)).then_inc(tables_in, 16)
            for i, v in enumerate((q_b, k_b)):
                sp.dma_start(ln_b[:, i, :], v.partition_broadcast(P)).then_inc(tables_in, 16)
            sp.dma_start(cos_sb[:], cos.rearrange("(t p) d -> p t d", p=P)).then_inc(tables_in, 16)
            sp.dma_start(sin_sb[:], sin.rearrange("(t p) d -> p t d", p=P)).then_inc(tables_in, 16)
            for s in (w_in_sem, wo_in, fc_in, pj_in):
                sp.sem_inc(s.sem, 1)
            with sp.Fori(0, KV) as g:
                def load_w(c):
                    sp.dma_start(w_raw[:], w_in[bass.ds(g, 1), c].rearrange("o p n -> p (o n)"))\
                        .then_inc(w_in_sem.sem, 16)

                def load_fc(e):
                    sp.dma_start(fc_raw[:], w_fc[bass.ds(g, 1), e].rearrange("o (a p) n -> p (o a) n", p=P))\
                        .then_inc(fc_in.sem, 16)

                def load_proj(e):
                    sp.dma_start(pj_sb[:], w_proj[bass.ds(g, 1), e].rearrange("o (a p) n -> p (o a) n", p=P))\
                        .then_inc(pj_in.sem, 16)

                wait(sp, w_hi_done, g, 0)
                wait(sp, w_lo_done, g, 0)
                load_w(0)
                wait(sp, fc_hi_done, g, 0)
                wait(sp, fc_lo_done, g, 0)
                load_fc(0)
                wait(sp, w_hi_done, g, 1)
                wait(sp, w_lo_done, g, 1)
                load_w(1)
                wait(sp, filled, g, 0)
                load_proj(0)
                sp.dma_start(wo_sb[:], w_o[bass.ds(g, 1)].rearrange("o (h p) n -> p (o h) n", p=P))\
                    .then_inc(wo_in.sem, 16)
                wait(sp, fc_hi_done, g, 1)
                wait(sp, fc_lo_done, g, 1)
                load_fc(1)
                wait(sp, filled, g, number["fill", ("Y", 3, 1)])
                load_proj(1)
            out_tiles = out.rearrange("(t p) c -> p t c", p=P)
            sp.wait_ge(acc_done.sem, 1 + KV * acc_done.per)
            for q in range(4):
                sp.dma_start(out_tiles[:, 4 * q:4 * q + 4, :], acc[:, 4 * q:4 * q + 4, :]).then_inc(stored, 16)
            sp.wait_ge(stored, 64)

        @block.gpsimd
        def _(pool):
            for s in (rstd_done, bias_parts, tables_done, swap_done):
                pool.sem_inc(s.sem, 1)
            pool.memset(minus_half[:], -0.5).then_inc(pre_pool, 1)
            for e in range(E):
                pool.memset(rank[:, e:e + 1], float(E - e)).then_inc(pre_pool, 1)
            pool.wait_ge(pre_pool, 1 + E)
            pool.wait_ge(pre_dve, 2 * T)
            pool.tensor_scalar(x_var, x_mv[:, :, 1], LN_EPS, None, ALU.add).then_inc(pre_pool, 1)
            pool.wait_ge(pre_pool, 2 + E)
            pool.tensor_tensor(x_rstd, x_var, minus_half[:], ALU.pow).then_inc(pre_pool, 1)
            pool.wait_ge(tables_in, 96)
            pool.tensor_scalar(ln_w[:, 0, :], ln_w[:, 0, :], D ** -0.5, None, ALU.mult).then_inc(pre_pool, 1)
            pool.tensor_scalar(ln_b[:, 0, :], ln_b[:, 0, :], D ** -0.5, None, ALU.mult).then_inc(pre_pool, 1)
            pool.wait_ge(pre_pool, 5 + E)
            for full, swapped in ((ln_w, ln_ws), (ln_b, ln_bs)):
                pool.tensor_scalar(swapped[:, :, 0:64], full[:, :, 64:128], -1.0, None, ALU.mult)
                pool.tensor_scalar(swapped[:, :, 64:128], full[:, :, 0:64], 1.0, None, ALU.mult)\
                    .then_inc(pre_pool, 1)
            pool.wait_ge(pre_pool, 7 + E)

            def halves(ap):
                return ap.rearrange("p a (b d) -> p (a b) d", b=2)

            def tables(g, t):
                cos_t = cos_sb[:, t:t + 1, :].to_broadcast([P, 4, D // 2])
                sin_t = sin_sb[:, t:t + 1, :].to_broadcast([P, 4, D // 2])
                wait(pool, same_done, g, t)
                wait(pool, swap_done, g, t)
                wait(pool, rotated_done, g, t)
                pool.tensor_tensor(halves(table_same[:]), halves(ln_w[:]), cos_t, ALU.mult)
                pool.tensor_tensor(halves(table_swap[:]), halves(ln_ws[:]), sin_t, ALU.mult)
                pool.tensor_tensor(halves(table_bias[:]), halves(ln_b[:]), cos_t, ALU.mult)
                pool.tensor_tensor(halves(bias_part), halves(ln_bs[:]), sin_t, ALU.mult)\
                    .then_inc(bias_parts.sem, 1)
                wait(pool, bias_parts, g, t + 1)
                pool.tensor_tensor(table_bias[:], table_bias[:], bias_part, ALU.add)\
                    .then_inc(tables_done.sem, 1)

            with pool.Fori(0, KV) as g:
                for kind, t in order["pool"]:
                    if kind == "tables":
                        tables(g, t)
                    elif kind == "swap":
                        wait(pool, qkv_read, g, 3 * t + 2)
                        wait(pool, tables_done, g, t + 1)
                        for heads, i in ((slice(0, HG), 0), (slice(HG, HG + 1), 1)):
                            n = heads.stop - heads.start
                            for a, b in ((slice(0, 64), slice(64, 128)), (slice(64, 128), slice(0, 64))):
                                ins = pool.tensor_tensor(
                                    t_swap[:, heads, a], qk_raw[:, heads, b],
                                    table_swap[:, i:i + 1, a].to_broadcast([P, n, 64]), ALU.mult)
                        ins.then_inc(swap_done.sem, 1)
                    elif kind == "rstd":
                        wait(pool, variance_done, g, t + 1)
                        wait(pool, rotated_done, g, t)
                        pool.tensor_tensor(rstd[:], variance[:], minus_half[:, 0:HG + 1], ALU.pow)\
                            .then_inc(rstd_done.sem, 1)

        @block.scalar
        def _(act):
            for s in (w_hi_done, fc_hi_done, qkv_read, gate_done, qk_hi_done, exp_done, pt_hi_done,
                      o_copied, relu_done, hidden_done, gated):
                act.sem_inc(s.sem, 1)
            act.wait_ge(consts_in, 48)
            act.activation(wr_hi[:], wr_raw, ACT.Copy).then_inc(pre_act, 1)
            act.activation(ident_b[:], ident_f[:], ACT.Copy).then_inc(pre_act, 1)
            act.activation(mask_b[:], mask_f, ACT.Copy).then_inc(pre_act, 1)
            for i in range(CT * 4):
                act.wait_ge(pre_pe, i + 1)
                act.activation(xT_hi[:, i % 2, (i // 2) * CHUNK:(i // 2 + 1) * CHUNK], banks[i % 4][:],
                               ACT.Copy).then_inc(pre_act, 1)
            act.wait_ge(pre_dve, 3 * T + 1 + 8 + 10)
            act.activation(rs[3], rs[2], ACT.Exp).then_inc(pre_act, 1)

            with act.Fori(0, KV) as g:
                for step in order["act"]:
                    kind, a = step[0], step[1:]
                    if kind == "w_high":
                        c = a[0]
                        wait(act, mean_step, g, 3 * c + 3)
                        wait(act, filled, g, 0)
                        act.activation(w_hi[:, c, :], w_raw[:], ACT.Copy).then_inc(w_hi_done.sem, 1)
                    elif kind == "fc_hi":
                        e = a[0]
                        wait(act, fc_in, g, e + 1)
                        wait(act, filled, g, number["fill", ("H", 4 * e - 1, 1)] if e else 0)
                        act.activation(fc_hi[:], fc_raw[:], ACT.Copy).then_inc(fc_hi_done.sem, 1)
                    elif kind == "relu":
                        m, d = a
                        wait_filled(act, g, "H", m, d)
                        if d == 0:
                            wait(act, filled, g, number["fill", ("Y", m - 1, 1)] if m else 0)
                        act.activation(hidden[:, d, :], bank("H", m, d)[:], ACT.Relu).then_inc(relu_done.sem, 1)
                    elif kind == "square":
                        m = a[0]
                        wait(act, relu_done, g, 2 * m + 2)
                        act.activation(hidden[:], hidden[:], ACT.Square).then_inc(hidden_done.sem, 1)
                    elif kind == "q_take":
                        t = a[0]
                        wait_filled(act, g, "Q", t)
                        wait(act, same_done, g, t)
                        wait(act, swap_done, g, t)
                        wait(act, filled, g, number["fill", ("KT", t - 1)] if t else 0)
                        act.activation(qk_raw[:, 0:HG, :], bank("Q", t)[:], ACT.Copy)
                        act.activation(squares[:, 0:HG, :], bank("Q", t)[:], ACT.Square)\
                            .then_inc(qkv_read.sem, 1)
                    elif kind == "kv_take":
                        t = a[0]
                        wait_filled(act, g, "KV", t)
                        act.activation(qk_raw[:, HG, :], bank("KV", t)[:, 0:D], ACT.Copy)
                        act.activation(squares[:, HG, :], bank("KV", t)[:, 0:D], ACT.Square)\
                            .then_inc(qkv_read.sem, 1)
                        act.activation(v_hi[:, t, :], bank("KV", t)[:, D:2 * D], ACT.Copy)\
                            .then_inc(qkv_read.sem, 1)
                    elif kind == "tanh":
                        t = a[0]
                        wait_filled(act, g, "G", t)
                        wait(act, filled, g, number["fill", ("GT", t - 2)] if t >= 2 else 0)
                        act.activation(gate[:, t % 2, :], bank("G", t)[:], ACT.Tanh, scale=0.5)\
                            .then_inc(gate_done.sem, 1)
                    elif kind == "q_hi":
                        t = a[0]
                        wait_filled(act, g, "QT", t)
                        act.activation(qT_hi[:], bank("QT", t)[:], ACT.Copy).then_inc(qk_hi_done.sem, 1)
                    elif kind == "k_hi":
                        t = a[0]
                        wait_filled(act, g, "KT", t)
                        act.activation(kT_hi[:, t * P:(t + 1) * P], bank("KT", t)[:, 0:P], ACT.Copy)\
                            .then_inc(qk_hi_done.sem, 1)
                    elif kind == "exp":
                        t, h, c = a
                        u, w = (2 * t + h // 2) % 2, chunks_of(t)[c]
                        if h % 2 == 0 and c == 0 and t:
                            wait(act, pt_filled, g, number["turn_probs", t - 1, h // 2, (t + 1) // 2 - 1])
                        if h == 0 and c == 0 and t >= 2:
                            wait(act, sum_step, g, 2 * (t - 2) + 1)
                        wait(act, neg_max_done, g, HG * t + h + 1)
                        act.activation(probs[:, u, h % 2, c * CHUNK:c * CHUNK + w], bank("scores", t, h, c)[:, 0:w],
                                       ACT.Exp, bias=neg_max[:, u, h % 2:h % 2 + 1],
                                       accum_out=chunk_sum[:, t % 2, h, c:c + 1]).then_inc(exp_done.sem, 1)
                    elif kind == "gate_scale":
                        t = a[0]
                        wait(act, inv_done, g, t + 1)
                        wait(act, gate_done, g, t + 1)
                        for h in range(HG):
                            gh, inv = gate[:, t % 2, h * D:(h + 1) * D], half_inv[:, h:h + 1]
                            ins = act.activation(gh, gh, ACT.Identity, bias=inv, scale=inv)
                        ins.then_inc(gated.sem, 1)
                    elif kind == "p_hi":
                        t, p, i = a
                        n = number[step]
                        w = 256 * min(2, t + 1 - 2 * i)
                        wait(act, pt_filled, g, n)
                        wait(act, pv_done, g, n - PT_RING)
                        act.activation(pT_hi[:, n % PT_RING, 0:w], pt_bank[n % 2][:, 0:w], ACT.Copy)\
                            .then_inc(pt_hi_done.sem, 1)
                    elif kind == "o_take":
                        t, p = a
                        wait(act, pv_done, g, number["pv", t, p, (t + 2) // 2 - 1])
                        wait(act, og_done, g, t)
                        act.activation(oT[:, 256 * p:256 * p + 256], o_bank[:, 256 * p:256 * p + 256],
                                       ACT.Copy).then_inc(o_copied.sem, 1)

        @block.vector
        def _(dve):
            for s in (mean_step, variance_done, w_lo_done, fc_lo_done, wtok_done, v_lo_done, sumsq_done, same_done, both_done,
                      rotated_done, qk_lo_done, chunk_max_done, neg_max_done, pt_lo_done, sum_step, inv_done,
                      og_done, acc_done):
                dve.sem_inc(s.sem, 1)
            for t in range(T):
                dve.wait_ge(x_in, 16 * 4)
                dve.bn_stats(x_stats[:, t, :], acc[:, t, :]).then_inc(pre_dve, 1)
            for t in range(T):
                dve.wait_ge(pre_dve, t + 1)
                dve.bn_aggr(x_mv[:, t, :], x_stats[:, t, :]).then_inc(pre_dve, 1)
            dve.wait_ge(pre_pool, 3 + E)
            dve.wait_ge(pre_dve, 2 * T)
            for t in range(T):
                dve.tensor_scalar(xn[:, t, :], acc[:, t, :], x_mv[:, t, 0:1], x_rstd[:, t:t + 1],
                                  ALU.subtract, ALU.mult).then_inc(pre_dve, 1)
            dve.wait_ge(pre_act, 1)
            dve.tensor_tensor(wr_lo[:], wr_raw, wr_hi[:].bitcast(F32), ALU.subtract).then_inc(pre_dve, 1)
            for i in range(CT * 4):
                dve.wait_ge(pre_act, 3 + i + 1)
                cols = slice((i // 2) * CHUNK, (i // 2 + 1) * CHUNK)
                dve.tensor_tensor(xT_lo[:, i % 2, cols], banks[i % 4][:], xT_hi[:, i % 2, cols].bitcast(F32),
                                  ALU.subtract).then_inc(pre_dve, 1)
            n0 = 3 * T + 1 + CT * 4
            logit, pick0, rest, pick1 = rt
            top0, r_a, diff, ex, p1, p0 = rs
            done = n0

            def link(ins):
                nonlocal done
                done += 1
                ins.then_inc(pre_dve, 1)
                dve.wait_ge(pre_dve, done)

            def over_experts(ap):
                return ap.unsqueeze(2).to_broadcast([P, T, E])

            rank_all = rank.unsqueeze(1).to_broadcast([P, T, E])
            dve.wait_ge(pre_pe, CT * 4 + 1)
            link(dve.tensor_copy(logit.rearrange("p t e -> p (t e)"), banks[4][:, 0:T * E]))
            link(dve.tensor_reduce(top0, logit, AX.X, ALU.max))
            link(dve.tensor_tensor(rest, logit, over_experts(top0), ALU.is_equal))
            link(dve.tensor_tensor(rest, rest, rank_all, ALU.mult))
            link(dve.tensor_reduce(r_a, rest, AX.X, ALU.max))
            link(dve.tensor_tensor(pick0, rank_all, over_experts(r_a), ALU.is_equal))
            link(dve.scalar_tensor_tensor(rest, pick0, MASKED, logit, ALU.mult, ALU.add))
            link(dve.tensor_reduce(r_a, rest, AX.X, ALU.max))
            link(dve.tensor_tensor(pick1, rest, over_experts(r_a), ALU.is_equal))
            link(dve.tensor_tensor(diff, r_a, top0, ALU.subtract))
            assert done == 3 * T + 1 + 8 + 10
            link(dve.tensor_tensor(pick1, pick1, rank_all, ALU.mult))
            link(dve.tensor_reduce(r_a, pick1, AX.X, ALU.max))
            link(dve.tensor_tensor(pick1, rank_all, over_experts(r_a), ALU.is_equal))
            dve.wait_ge(pre_act, 3 + CT * 4 + 1)
            link(dve.tensor_scalar(p1, ex, 1.0, None, ALU.add))
            link(dve.reciprocal(p0, p1))
            link(dve.tensor_tensor(p1, ex, p0, ALU.mult))
            link(dve.tensor_tensor(pick0, pick0, over_experts(p0), ALU.mult))
            link(dve.tensor_tensor(pick1, pick1, over_experts(p1), ALU.mult))
            link(dve.tensor_tensor(w_tok[:].rearrange("p e t -> p t e"), pick0, pick1, ALU.add))

            with dve.Fori(0, KV) as g:
                wait(dve, acc_done, g, 0)
                dve.tensor_copy(w_tok_g[:], w_tok[:, bass.ds(g * EG, EG), :]).then_inc(wtok_done.sem, 1)
                for step in order["dve"]:
                    kind, a = step[0], step[1:]
                    if kind == "centre":
                        c = a[0]
                        qk = w_raw[:, 0:QW + D].rearrange("p (h d) -> p h d", d=D)
                        wait(dve, w_in_sem, g, c + 1)
                        dve.tensor_reduce(head_sum[:], qk, AX.X, ALU.add).then_inc(mean_step.sem, 1)
                        wait(dve, mean_step, g, 3 * c + 1)
                        dve.tensor_scalar(head_mean[:], head_sum[:], 1.0 / D, None, ALU.mult)\
                            .then_inc(mean_step.sem, 1)
                        wait(dve, mean_step, g, 3 * c + 2)
                        dve.tensor_tensor(qk, qk, head_mean[:].unsqueeze(2).to_broadcast([P, HG + 1, D]),
                                          ALU.subtract).then_inc(mean_step.sem, 1)
                    elif kind == "w_low":
                        c = a[0]
                        wait(dve, w_hi_done, g, c + 1)
                        dve.tensor_tensor(w_lo[:, c, :], w_raw[:], w_hi[:, c, :].bitcast(F32), ALU.subtract)\
                            .then_inc(w_lo_done.sem, 1)
                    elif kind == "fc_lo":
                        wait(dve, fc_hi_done, g, a[0] + 1)
                        dve.tensor_tensor(fc_lo[:], fc_raw[:], fc_hi[:].bitcast(F32), ALU.subtract)\
                            .then_inc(fc_lo_done.sem, 1)
                    elif kind == "y_add":
                        m, half = a
                        if m == 0 and half == 0:
                            wait(dve, wtok_done, g, 1)
                        wait_filled(dve, g, "Y", m, half)
                        for k in range(2):
                            tile = (m % 4) * 4 + 2 * half + k
                            n = acc_number[step] - 1 + k
                            wait(dve, acc_done, g, acc_before[n])
                            dve.scalar_tensor_tensor(
                                acc[:, tile, :], bank("Y", m, half)[:, k * C:(k + 1) * C],
                                w_tok_g[:, m // 4, tile:tile + 1], acc[:, tile, :], ALU.mult, ALU.add)\
                                .then_inc(acc_done.sem, 1)
                    elif kind == "sumsq":
                        t = a[0]
                        wait(dve, qkv_read, g, 3 * t + 2)
                        dve.tensor_reduce(sumsq[:], squares[:], AX.X, ALU.add).then_inc(sumsq_done.sem, 1)
                        wait(dve, sumsq_done, g, t + 1)
                        dve.tensor_scalar(variance[:], sumsq[:], 1.0 / D, QK_EPS, ALU.mult, ALU.add)\
                            .then_inc(variance_done.sem, 1)
                    elif kind == "same":
                        t = a[0]
                        wait(dve, tables_done, g, t + 1)
                        wait(dve, rotated_done, g, t)
                        dve.tensor_tensor(t_same[:, HG, :], qk_raw[:, HG, :], table_same[:, 1, :], ALU.mult)
                        dve.tensor_tensor(t_same[:, 0:HG, :], qk_raw[:, 0:HG, :],
                                          table_same[:, 0:1, :].to_broadcast([P, HG, D]), ALU.mult)\
                            .then_inc(same_done.sem, 1)
                    elif kind == "v_lo":
                        t = a[0]
                        wait(dve, qkv_read, g, 3 * t + 3)
                        dve.tensor_tensor(v_lo[:, t, :], bank("KV", t)[:, D:2 * D], v_hi[:, t, :].bitcast(F32),
                                          ALU.subtract).then_inc(v_lo_done.sem, 1)
                    elif kind == "rope_b":
                        t = a[0]
                        wait(dve, swap_done, g, t + 1)
                        wait(dve, same_done, g, t + 1)
                        dve.tensor_tensor(t_same[:], t_same[:], t_swap[:], ALU.add).then_inc(both_done.sem, 1)
                        wait(dve, both_done, g, t + 1)
                        wait(dve, rstd_done, g, t + 1)
                        for h in range(HG + 1):
                            ins = dve.scalar_tensor_tensor(rotated[:, h, :], t_same[:, h, :], rstd[:, h:h + 1],
                                                           table_bias[:, h // HG, :], ALU.mult, ALU.add)
                        ins.then_inc(rotated_done.sem, 1)
                    elif kind == "q_lo":
                        t = a[0]
                        wait(dve, qk_hi_done, g, 2 * t + 1)
                        dve.tensor_tensor(qT_lo[:], bank("QT", t)[:], qT_hi[:].bitcast(F32), ALU.subtract)\
                            .then_inc(qk_lo_done.sem, 1)
                    elif kind == "k_lo":
                        t = a[0]
                        wait(dve, qk_hi_done, g, 2 * t + 2)
                        cols = slice(t * P, (t + 1) * P)
                        dve.tensor_tensor(kT_lo[:, cols], bank("KT", t)[:, 0:P], kT_hi[:, cols].bitcast(F32),
                                          ALU.subtract).then_inc(qk_lo_done.sem, 1)
                    elif kind == "max":
                        t, h, c = a
                        u, w, n = (2 * t + h // 2) % 2, chunks_of(t)[c], len(chunks_of(t))
                        if c == 0 and t:
                            wait(dve, exp_done, g, number["exp", t - 1, h, len(chunks_of(t - 1)) - 1])
                        wait_filled(dve, g, "scores", t, h, c)
                        nm = neg_max[:, u, h % 2:h % 2 + 1]
                        if n == 1:
                            dve.tensor_reduce(nm, bank("scores", t, h, c)[:, 0:w], AX.X, ALU.max, negate=True)\
                                .then_inc(neg_max_done.sem, 1)
                        else:
                            dve.tensor_reduce(neg_chunk_max[:, u, h % 2, c:c + 1], bank("scores", t, h, c)[:, 0:w],
                                              AX.X, ALU.max, negate=True).then_inc(chunk_max_done.sem, 1)
                            if c == n - 1:
                                wait(dve, chunk_max_done, g, number[step] - (total["scores"] - n_many))
                                dve.tensor_reduce(nm, neg_chunk_max[:, u, h % 2, 0:n], AX.X, ALU.min)\
                                    .then_inc(neg_max_done.sem, 1)
                    elif kind == "p_lo":
                        t, p, i = a
                        n = number[step]
                        w = 256 * min(2, t + 1 - 2 * i)
                        wait(dve, pt_hi_done, g, n)
                        dve.tensor_tensor(pT_lo[:, n % PT_RING, 0:w], pt_bank[n % 2][:, 0:w],
                                          pT_hi[:, n % PT_RING, 0:w].bitcast(F32), ALU.subtract)\
                            .then_inc(pt_lo_done.sem, 1)
                    elif kind == "inv":
                        t = a[0]
                        n = len(chunks_of(t))
                        wait(dve, exp_done, g, number["exp", t, HG - 1, n - 1])
                        dve.tensor_reduce(row_sum[:], chunk_sum[:, t % 2, :, 0:n], AX.X, ALU.add)\
                            .then_inc(sum_step.sem, 1)
                        wait(dve, sum_step, g, 2 * t + 1)
                        dve.tensor_scalar(twice_sum[:], row_sum[:], 2.0, None, ALU.mult).then_inc(sum_step.sem, 1)
                        wait(dve, sum_step, g, 2 * t + 2)
                        wait(dve, gated, g, t)
                        dve.reciprocal(half_inv[:], twice_sum[:]).then_inc(inv_done.sem, 1)
                    elif kind == "og":
                        t = a[0]
                        wait_filled(dve, g, "GT", t)
                        wait(dve, o_copied, g, 2 * t + 2)
                        wait(dve, filled, g, number["fill", ("OUT", t - 1)] if t else 0)
                        dve.tensor_tensor(ogT[:], bank("GT", t)[:], oT[:], ALU.mult)\
                            .then_inc(og_done.sem, 1)
                    elif kind == "out_add":
                        t = a[0]
                        wait_filled(dve, g, "OUT", t)
                        n = acc_number[step]
                        wait(dve, acc_done, g, acc_before[n])
                        dve.tensor_tensor(acc[:, t, :], bank("OUT", t)[:, 0:C], acc[:, t, :], ALU.add)\
                            .then_inc(acc_done.sem, 1)

        @block.tensor
        def _(pe):
            for s in (filled, pt_filled, pv_done):
                pe.sem_inc(s.sem, 1)
            pe.wait_ge(consts_in, 48)
            for i in range(CT * 4):
                if i >= 4:
                    pe.wait_ge(pre_dve, 3 * T + 1 + i - 3)
                for k in range(4):
                    t = 4 * (i // 2) + k
                    pe.wait_ge(pre_dve, 2 * T + t + 1)
                    ins = pe.transpose(banks[i % 4][:, k * P:(k + 1) * P], xn[:, t, (i % 2) * P:(i % 2 + 1) * P],
                                       ident_f[:])
                ins.then_inc(pre_pe, 1)
            pe.wait_ge(pre_dve, 3 * T + 1 + CT * 4)
            for t in range(T):
                rows = slice(t * P, (t + 1) * P)
                todo = [(xs, ws, c) for c in range(CT) for xs, ws in
                        ((xT_hi, wr_hi), (xT_hi, wr_lo), (xT_lo, wr_hi))]
                for n, (xs, ws, c) in enumerate(todo):
                    ins = pe.matmul(banks[4][:, t * E:(t + 1) * E], xs[:, c, rows], ws[:, c, :],
                                    start=(n == 0), stop=(n == len(todo) - 1))
            ins.then_inc(pre_pe, 1)
            pe.wait_ge(pre_dve, 3 * T + 1 + CT * 4 + 1)
            pe.wait_ge(pre_act, 3 + CT * 4)

            def three(out_ap, stationary, moving, start=True, stop=True):
                n, last = len(stationary), 3 * len(stationary)
                done = 0
                for (s_hi, s_lo), (m_hi, m_lo) in zip(stationary, moving):
                    for s, m in ((s_hi, m_hi), (s_hi, m_lo), (s_lo, m_hi)):
                        done += 1
                        ins = pe.matmul(out_ap, s, m, start=(start and done == 1), stop=(stop and done == last))
                return ins

            with pe.Fori(0, KV) as g:
                for step in order["pe"]:
                    kind, a = step[0], step[1:]
                    if kind in FILLS:
                        wait_bank_free(pe, g, *step)
                    if kind == "H":
                        m, d = a
                        cols, ds = slice((m % 4) * CHUNK, (m % 4 + 1) * CHUNK), slice(d * P, (d + 1) * P)
                        if m % 4 == 0 and d == 0:
                            wait(pe, fc_lo_done, g, m // 4 + 1)
                        three(bank("H", m, d)[:], [(fc_hi[:, c, ds], fc_lo[:, c, ds]) for c in range(CT)],
                              [(xT_hi[:, c, cols], xT_lo[:, c, cols]) for c in range(CT)])\
                            .then_inc(filled.sem, 1)
                    elif kind == "Y":
                        m, half = a
                        if m % 4 == 0 and half == 0:
                            wait(pe, pj_in, g, m // 4 + 1)
                        wait(pe, hidden_done, g, m + 1)
                        for k in range(2):
                            for d in range(2):
                                cols = slice((2 * half + k) * P, (2 * half + k + 1) * P)
                                ins = pe.matmul(bank("Y", m, half)[:, k * C:(k + 1) * C], hidden[:, d, cols],
                                                pj_sb[:, d, :], start=(d == 0), stop=(d == 1))
                        ins.then_inc(filled.sem, 1)
                    elif kind in ("Q", "KV", "G"):
                        t = a[0]
                        rows = slice(t * P, (t + 1) * P)
                        cols = {"Q": slice(0, QW), "KV": slice(QW, QW + 2 * D), "G": slice(QW + 2 * D, WCOLS)}[kind]
                        if t == 0 and kind == "Q":
                            wait(pe, w_lo_done, g, CT)
                        three(bank(kind, t)[:, 0:cols.stop - cols.start],
                              [(xT_hi[:, c, rows], xT_lo[:, c, rows]) for c in range(CT)],
                              [(w_hi[:, c, cols], w_lo[:, c, cols]) for c in range(CT)]).then_inc(filled.sem, 1)
                    elif kind == "QT":
                        t = a[0]
                        wait(pe, rotated_done, g, t + 1)
                        for h in range(HG):
                            ins = pe.transpose(bank("QT", t)[:, h * P:(h + 1) * P], rotated[:, h, :], ident_f[:])
                        ins.then_inc(filled.sem, 1)
                    elif kind == "KT":
                        t = a[0]
                        pe.transpose(bank("KT", t)[:, 0:P], rotated[:, HG, :], ident_f[:]).then_inc(filled.sem, 1)
                    elif kind == "scores":
                        t, h, c = a
                        w = chunks_of(t)[c]
                        if h == 0 and c == 0:
                            wait(pe, qk_lo_done, g, 2 * t + 2)
                        heads, keys = slice(h * P, (h + 1) * P), slice(c * CHUNK, c * CHUNK + w)
                        diagonal = c == len(chunks_of(t)) - 1
                        ins = three(bank("scores", t, h, c)[:, 0:w],
                                    [(qT_hi[:, heads], qT_lo[:, heads])],
                                    [(kT_hi[:, keys], kT_lo[:, keys])], stop=not diagonal)
                        if diagonal:
                            ins = pe.matmul(bank("scores", t, h, c)[:, w - P:w], ident_b[:], mask_b[:],
                                            start=False, stop=True)
                        ins.then_inc(filled.sem, 1)
                    elif kind == "turn_probs":
                        t, p, i = a
                        n = number[step]
                        wait(pe, exp_done, g, max(number["exp", t, 2 * p + hh, min(2 * i + 1, t) // 4]
                                                  for hh in range(2)))
                        wait(pe, pt_lo_done, g, n - 2)
                        for jj in range(min(2, t + 1 - 2 * i)):
                            for hh in range(2):
                                j = 2 * i + jj
                                ins = pe.transpose(pt_bank[n % 2][:, (2 * jj + hh) * P:(2 * jj + hh + 1) * P],
                                                   probs[:, (2 * t + p) % 2, hh, j * P:(j + 1) * P], ident_f[:])
                        ins.then_inc(pt_filled.sem, 1)
                    elif kind == "pv":
                        t, p, i = a
                        n = number[step]
                        wait(pe, pt_lo_done, g, n)
                        if i == 0:
                            wait(pe, o_copied, g, 2 * t + p)
                            wait(pe, v_lo_done, g, t + 1)
                        for jj in range(min(2, t + 1 - 2 * i)):
                            j, cols = 2 * i + jj, slice(2 * jj * P, 2 * (jj + 1) * P)
                            ins = three(o_bank[:, 256 * p:256 * p + 256], [(v_hi[:, j, :], v_lo[:, j, :])],
                                        [(pT_hi[:, n % PT_RING, cols], pT_lo[:, n % PT_RING, cols])],
                                        start=(j == 0), stop=(j == t))
                        ins.then_inc(pv_done.sem, 1)
                    elif kind == "GT":
                        t = a[0]
                        wait(pe, gated, g, t + 1)
                        for h in range(HG):
                            ins = pe.transpose(bank("GT", t)[:, h * P:(h + 1) * P],
                                               gate[:, t % 2, h * D:(h + 1) * D], ident_f[:])
                        ins.then_inc(filled.sem, 1)
                    elif kind == "OUT":
                        t = a[0]
                        wait(pe, og_done, g, t + 1)
                        if t == 0:
                            wait(pe, wo_in, g, 1)
                        for h in range(HG):
                            ins = pe.matmul(bank("OUT", t)[:, 0:C], ogT[:, h * P:(h + 1) * P], wo_sb[:, h, :],
                                            start=(h == 0), stop=(h == HG - 1))
                        ins.then_inc(filled.sem, 1)


def kernel(L0_attn_x, L0_attn_w_qkv, L0_attn_w_o, L0_attn_q_norm_w, L0_attn_q_norm_b, L0_attn_k_norm_w,
           L0_attn_k_norm_b, L0_ffn_w_router, L0_ffn_w_fc, L0_ffn_w_proj):
    import concourse.bacc as bacc
    from concourse.bass_utils import run_bass_kernel_spmd

    pairs = np.concatenate([np.arange(0, D, 2), np.arange(1, D, 2)])
    w = np.asarray(L0_attn_w_qkv)
    wq = w[0:H * D].reshape(KV, HG, D, C)[:, :, pairs].reshape(KV, HG * D, C)
    wg = w[H * D:2 * H * D].reshape(KV, HG * D, C)
    wk = w[2 * H * D:2 * H * D + KV * D].reshape(KV, D, C)[:, pairs]
    wv = w[2 * H * D + KV * D:].reshape(KV, D, C)
    w_in = np.concatenate([wq, wk, wv, wg], axis=1).transpose(0, 2, 1).reshape(KV, CT, P, WCOLS)
    inv = np.float32(1.0) / np.power(np.float32(ROPE_BASE), np.arange(0, D, 2, dtype=np.float32) / np.float32(D))
    angles = np.outer(np.arange(S, dtype=np.float32), inv.astype(np.float32)).astype(np.float32)
    arrays = {
        "x": np.asarray(L0_attn_x).reshape(S, C),
        "w_in": w_in,
        "w_o": np.asarray(L0_attn_w_o).T.reshape(KV, HG * D, C),
        "q_w": np.asarray(L0_attn_q_norm_w)[pairs],
        "q_b": np.asarray(L0_attn_q_norm_b)[pairs],
        "k_w": np.asarray(L0_attn_k_norm_w)[pairs],
        "k_b": np.asarray(L0_attn_k_norm_b)[pairs],
        "w_router": np.asarray(L0_ffn_w_router),
        "w_fc": np.asarray(L0_ffn_w_fc).reshape(KV, EG, C, C),
        "w_proj": np.asarray(L0_ffn_w_proj).reshape(KV, EG, C, C),
        "cos": np.cos(angles),
        "sin": np.sin(angles),
        "ident": np.eye(P, dtype=np.float32),
        "mask": np.triu(np.full((P, P), MASKED, np.float32), 1),
    }
    arrays = {n: np.ascontiguousarray(a) for n, a in arrays.items()}
    nc = bacc.Bacc("TRN2", target_bir_lowering=False, num_devices=1)
    args = [nc.dram_tensor(f"in_{n}", a.shape, mybir.dt.from_np(a.dtype), kind="ExternalInput").ap()
            for n, a in arrays.items()]
    args.append(nc.dram_tensor("out_0", (S, C), F32, kind="ExternalOutput").ap())
    build(nc, *args)
    r = run_bass_kernel_spmd(nc, [{f"in_{n}": a for n, a in arrays.items()}], core_ids=[0])
    return r.results[0]["out_0"].reshape(1, S, C)
```

```python
from contextlib import ExitStack

import numpy as np

import concourse.bass as bass
from concourse import mybir

F32 = mybir.dt.float32
F32R = mybir.dt.float32r
BF16 = mybir.dt.bfloat16
ALU = mybir.AluOpType
ACT = mybir.ActivationFunctionType
AX = mybir.AxisListType

P = 128
S = 2048
C = 256
D = 128
H = 16
KV = 4
HG = H // KV
E = 8
T = S // P
CT = C // P
CHUNK = 512
ROPE_BASE = 1000000.0
LN_EPS = 1e-5
QK_EPS = 1e-6
MASKED = -3.0e38
NBANK = 5
PT_RING = 3
QW = HG * D
WCOLS = 2 * QW + 2 * D
EG = E // KV
JOBS = EG * (S // CHUNK)
SCORE_BANKS = {1: (0, 1, 2), 2: (0, 1, 2), 3: (0, 1, 2, 3), 4: (0, 1, 2, 3)}
OTHER_BANKS = {1: (1, 2, 3, 4), 2: (3, 4), 3: (4,), 4: (4,), "end": (0, 1, 2, 3, 4)}
FILLS = ("Q", "KV", "G", "QT", "KT", "GT", "OUT", "H", "Y", "scores")
HANDOVER = {"pe": (0.0, 0.2), "act": (0.28, 0.15), "dve": (0.2, 0.13), "pool": (0.3, 0.16), "sp": (0.2, 0.2)}
DUE = {"start": 45.11, "per_step": 1.46, "per_chunk": 0.96, "per_unit": -7.97, "rope": -6.76, "v_lo": -38.54,
       "rope_b": -77.02, "turn": -98.69, "gate": 9.8, "inv": -104.43, "scale": 80.69, "turn_gate": -58.01,
       "og": 8.15, "out": 36.23, "out_add": 72.2, "scores": -19.05, "max": 144.63, "exp": 11.55,
       "prob_step": 0.12, "pv": 23.27, "p_hi": 5.78, "p_lo": 45.38, "expert": 0.0, "expert_step": 15.0,
       "evict": 0.0, "evict_step": 20.0, "first_half": 0.78, "window": 0.02, "last_y": -2.41, "wo": 24.46,
       "og_hi": -25.19, "og_lo": 66.45, "next": -57.16, "next_w": -143.6}


def freed_by_step(step):
    kind, a = step[0], step[1:]
    return ({"Q": "q_take", "KV": "v_lo", "G": "tanh", "QT": "q_lo", "KT": "k_lo", "GT": "og", "OUT": "out_add",
             "scores": "exp", "H": "hid_lo", "Y": "y_add"}[kind], *a)


class Steps:

    def __init__(self, sem, per, unit=1, look_back=False):
        self.sem, self.per, self.unit = sem, per * unit, unit
        self.first = 1 + (self.per if look_back else 0)

    def after(self, g, n):
        return g * self.per + (self.first + n * self.unit)

    def after_before(self, g, n):
        return self.after(g, n - self.per // self.unit)


def chunks_of(t):
    width = (t + 1) * P
    return [min(CHUNK, width - c) for c in range(0, width, CHUNK)]


def due_times():
    begin, now = {}, DUE["start"]
    for t in range(T):
        for p in range(HG // 2):
            begin[t, p] = now
            now += DUE["per_step"] * ((t + 2) // 2) + DUE["per_chunk"] * len(chunks_of(t)) + DUE["per_unit"]
    begin[T, 0] = begin[T, 1] = now
    return begin


def group_steps():
    begin = due_times()
    steps = []

    def add(queue, step, cost, needs, due):
        steps.append((queue, step, cost, [n for n in needs if n is not None], due))

    def old(tile, *step):
        return step if tile >= 0 else None

    n = 0
    prob_steps = [(t, p, i) for t in range(T) for p in range(HG // 2) for i in range((t + 2) // 2)]
    for e in range(1, EG + 1):
        at = begin[T, 0] + DUE["next"] if e == EG else 60
        add("sp fc", ("fc_load", e), 2.5, [("pj_lo", e - 1) if e > 1 else None], 0)
        add("act fc", ("fc_hi", e), 0.55, [("fc_load", e), ("H", 4 * e - 1, 1)], at)
        add("dve fc", ("fc_lo", e), 0.6, [("fc_hi", e)], at)
        add("sp fc", ("pj_load", e), 2.5, [("fc_lo", e)], 0)
        add("act fc", ("pj_hi", e), 0.55, [("pj_load", e), ("Y", 4 * e - 1, 1)], at + 1)
        add("dve fc", ("pj_lo", e), 0.6, [("pj_hi", e)], at + 1)
    at = begin[T, 0] + DUE["next_w"]
    used = [(kind, T - 1) for kind in ("Q", "KV", "G")]
    add("act wo", ("wo_hi", 0), 0.95, [], DUE["wo"])
    add("dve wo", ("wo_lo", 0), 1.15, [("wo_hi", 0)], DUE["wo"])
    for c in range(CT):
        add("sp w", ("w_load", c), 2.5, [("w_low", c - 1) if c else ("wo_lo", 0)], 0)
        add("dve w", ("centre", c), 1.8, [("w_load", c)], at)
        add("act w", ("w_high", c), 1.15, [("centre", c)] + used, at)
        add("dve w", ("w_low", c), 1.4, [("w_high", c)], at)
    add("sp w", ("wo_load", 0), 2.5, [("w_low", CT - 1)], 0)
    for m in range(JOBS):
        at = DUE["expert"] + DUE["expert_step"] * m
        for d in range(2):
            add("pe H", ("H", m, d), 1.3,
                [("fc_lo", m // 4) if m >= 4 else None, ("Y", m - 1, 1) if m else None], at)
            add("act H", ("square", m, d), 1.1, [("H", m, d)], DUE["evict"] + DUE["evict_step"] * m)
            add("act H", ("hid_hi", m, d), 0.5, [("square", m, d), ("Y", m - 1, 1) if m else None],
                DUE["evict"] + DUE["evict_step"] * m)
            add("dve H", ("hid_lo", m, d), 0.65, [("hid_hi", m, d)], DUE["evict"] + DUE["evict_step"] * m)
        for half in range(2):
            at = begin[T, 0] + DUE["last_y"] if m == JOBS - 1 else DUE["expert"] + DUE["expert_step"] * m - 0.5
            add("pe Y", ("Y", m, half), 1.3, [("hid_lo", m, 1), ("pj_lo", m // 4) if m >= 4 else None], at)
            add("dve Y", ("y_add", m, half), 0.8, [("Y", m, half)], DUE["evict"] + DUE["evict_step"] * m - 10)
    for t in range(2, T + 2):
        add("sp angles", ("angle_load", t), 2.2, [("tables", t - 2)], 0)
    add("pool", ("tables", 0), 3.6, [], 0)
    for t in range(T):
        b0, b1, b2 = begin[t, 0], begin[t, 1], begin[t + 1, 0]
        add("pe QKV", ("Q", t), 1.3, [old(t - 1, "KT", t - 1)], b0 + DUE["rope"])
        add("pe QKV", ("KV", t), 0.65, [], b0 + DUE["rope"])
        add("pe G", ("G", t), 1.3, [old(t - 2, "GT", t - 2)], b1 + DUE["gate"])
        add("act QKV", ("q_take", t), 0.95, [("Q", t)] + [old(t - 1, x, t - 1) for x in ("same", "swap", "KT")],
            b0 + DUE["rope"])
        add("act QKV", ("kv_take", t), 0.5, [("KV", t)], b0 + DUE["rope"])
        add("dve rope", ("sumsq", t), 0.95, [("kv_take", t)], b0 + DUE["rope"])
        add("dve rope", ("same", t), 0.85, [("kv_take", t), ("tables", t), old(t - 1, "rope_b", t - 1)],
            b0 + DUE["rope"])
        add("dve v", ("v_lo", t), 0.2, [("kv_take", t)], b0 + DUE["v_lo"])
        add("pool", ("swap", t), 2.0, [("kv_take", t), old(t - 1, "rope_b", t - 1)], 0)
        add("pool", ("rstd", t), 1.2, [("sumsq", t)], 0)
        add("dve rope", ("rope_b", t), 2.2, [("swap", t), ("rstd", t)], b0 + DUE["rope_b"])
        if t + 1 < T:
            add("pool", ("tables", t + 1), 3.6, [("rope_b", t), ("same", t), ("angle_load", t + 1) if t else None], 0)
        last = len(chunks_of(t - 1)) - 1 if t else 0
        add("pe turn", ("QT", t), 0.43, [("rope_b", t), old(t - 1, "scores", t - 1, HG - 1, last)], b0 + DUE["turn"])
        add("pe turn", ("KT", t), 0.11, [("rope_b", t)], b0 + DUE["turn"])
        add("act turn", ("q_hi", t), 0.48, [("QT", t)], b0 + DUE["turn"])
        add("act turn", ("k_hi", t), 0.16, [("KT", t)], b0 + DUE["turn"])
        add("dve turn", ("q_lo", t), 0.6, [("q_hi", t)], b0 + DUE["turn"])
        add("dve turn", ("k_lo", t), 0.2, [("k_hi", t)], b0 + DUE["turn"])
        add("act gate", ("tanh", t), 0.48, [("G", t), old(t - 2, "GT", t - 2)], b1 + DUE["gate"])
        add("dve gate", ("inv", t), 0.5, [("exp", t, HG - 1, len(chunks_of(t)) - 1),
                                          old(t - 1, "gate_scale", t - 1)], b2 + DUE["inv"])
        add("act gate", ("gate_scale", t), 1.55, [("inv", t), ("tanh", t)], b2 + DUE["scale"])
        add("pe GT", ("GT", t), 0.43, [("gate_scale", t), ("o_take", t, 1), old(t - 1, "OUT", t - 1)],
            b2 + DUE["turn_gate"])
        add("dve out", ("og", t), 0.6, [("GT", t), ("o_take", t, 1)], b2 + DUE["og"])
        add("act og", ("og_hi", t), 0.48, [("og", t), old(t - 1, "OUT", t - 1)], b2 + DUE["og_hi"])
        add("dve og", ("og_lo", t), 0.6, [("og_hi", t)], b2 + DUE["og_lo"])
        add("pe OUT", ("OUT", t), 1.3, [("og_lo", t), ("wo_lo", 0)], b2 + DUE["out"])
        add("dve out", ("out_add", t), 0.33, [("OUT", t)], b2 + DUE["out_add"])
        for h in range(HG):
            p, hh = h // 2, h % 2
            start = begin[t, 0] if p == 0 else begin[t, 1]
            prev = begin[(t, 0) if p else (t - 1, 1)] if (t or p) else start - 6
            at = start - (start - prev) * (DUE["first_half"] if hh == 0 else 0.0)
            lag_exp = ("exp", t - 1, h, len(chunks_of(t - 1)) - 1) if t else None
            for c, w in enumerate(chunks_of(t)):
                add("pe S", ("scores", t, h, c), 3 * w / 2400 + 0.05, [("k_lo", t)], at + DUE["scores"])
                over_chunks = 0.2 if 0 < c == len(chunks_of(t)) - 1 else 0.0
                add("dve S", ("max", t, h, c), 0.07 + w / 960 + over_chunks, [("scores", t, h, c), lag_exp],
                    at + DUE["max"])
            for c, w in enumerate(chunks_of(t)):
                free = ("turn_probs", t - 1, p, (t + 1) // 2 - 1) if t else None
                add("act S", ("exp", t, h, c), 0.24 + w / 1200, [("max", t, h, len(chunks_of(t)) - 1), free,
                                                                 old(t - 2, "inv", t - 2)], at + DUE["exp"])
        for p in range(HG // 2):
            last = (t + 2) // 2 - 1
            for i in range(last + 1):
                two = min(2, t + 1 - 2 * i)
                d = begin[t, p] + DUE["prob_step"] * i
                old_p = [prob_steps[n - k] if n >= k else None for k in (2, 3)]
                exps = [("exp", t, 2 * p + hh, min(2 * i + 1, t) // 4) for hh in range(2)]
                add("pe PT", ("turn_probs", t, p, i), 0.215 * two,
                    exps + [("p_lo", *old_p[0]) if old_p[0] else None], d)
                add("act PT", ("p_hi", t, p, i), 0.05 + 0.215 * two,
                    [("turn_probs", t, p, i), ("pv", *old_p[1]) if old_p[1] else None], d + DUE["p_hi"])
                add("dve PT", ("p_lo", t, p, i), 0.07 + 0.265 * two, [("p_hi", t, p, i)], d + DUE["p_lo"])
                prev_take = (("o_take", t, p - 1) if p else old(t - 1, "o_take", t - 1, 1)) if i == 0 else None
                add("pe PV", ("pv", t, p, i), 0.325 * two, [("p_lo", t, p, i), ("v_lo", t), prev_take], d + DUE["pv"])
                n += 1
            add("act O", ("o_take", t, p), 0.27, [("pv", t, p, last), old(t - 1, "og_lo", t - 1)],
                begin[t, p] + DUE["prob_step"] * last)
    return steps


def plan_group():
    queues, cost, needs, due, on = {}, {}, {}, {}, {}
    for queue, step, c, need, when in group_steps():
        queues.setdefault(queue, []).append(step)
        cost[step], needs[step], due[step], on[step] = c, need, when, queue.split()[0]
    engines = {"pe": [], "act": [], "dve": [], "pool": [], "sp": []}
    clock = dict.fromkeys(engines, 0.0)
    done, bank_of, prior = {}, {}, {}
    held = [None] * NBANK
    width = [1]

    def bank_for(step):
        if step[0] == "scores":
            allowed = SCORE_BANKS[len(chunks_of(step[1]))]
        else:
            allowed = OTHER_BANKS[width[0]]
        free = []
        for b in allowed:
            if held[b] is None:
                free.append((0.0, b))
            elif freed_by_step(held[b]) in done:
                reader = freed_by_step(held[b])
                free.append((done[reader] + HANDOVER[on[reader]][0], b))
        return min(free) if free else None

    left = sum(len(q) for q in queues.values())
    while left:
        best = None
        for queue, waiting in queues.items():
            if not waiting:
                continue
            step, engine = waiting[0], queue.split()[0]
            if any(x not in done for x in needs[step]):
                continue
            start = max([0.0] + [done[x] + (HANDOVER[on[x]][engine != "pe"] if on[x] != engine else 0.0)
                                 for x in needs[step]])
            if step[0] in FILLS:
                free = bank_for(step)
                if free is None:
                    continue
                start = max(start, free[0])
            start = max(start, clock[engine])
            now = start <= clock[engine] + DUE["window"]
            key = (start if not now else clock[engine], due[step])
            if best is None or key < best[0]:
                best = (key, queue, step, engine, start)
        _, queue, step, engine, start = best
        queues[queue].pop(0)
        left -= 1
        if step[0] in FILLS:
            b = bank_for(step)[1]
            bank_of[step], prior[step], held[b] = b, held[b], step
            if step[0] == "scores":
                last_scores = step == ("scores", T - 1, HG - 1, len(chunks_of(T - 1)) - 1)
                width[0] = "end" if last_scores else len(chunks_of(step[1]))
        clock[engine] = done[step] = start + cost[step]
        engines[engine].append(step)
    return engines, bank_of, prior


def build(nc, x, w_in, w_o, q_w, q_b, k_w, k_b, w_router, w_fc, w_proj, cos_sin, ident, mask, out):
    order, bank_of, prior = plan_group()
    number, total = {}, {}
    for engine in order.values():
        for step in engine:
            total[step[0]] = total.get(step[0], 0) + 1
            number[step] = total[step[0]]
    for n, step in enumerate(bank_of):
        number["fill", step] = n + 1
    n_many = sum(len(chunks_of(t)) for t in range(T) if len(chunks_of(t)) > 1) * HG

    with ExitStack() as ctx:
        def sb(name, shape, dt=F32):
            return ctx.enter_context(nc.sbuf_tensor(name, shape, dt))

        def sem(name):
            return ctx.enter_context(nc.semaphore(name))

        acc = sb("acc", [P, T, C])
        xT_hi = sb("xT_hi", [P, CT, S], F32R)
        xT_lo = sb("xT_lo", [P, CT, S], F32R)
        w_raw = sb("w_raw", [P, WCOLS])
        w_hi = sb("w_hi", [P, CT, WCOLS], F32R)
        w_lo = sb("w_lo", [P, CT, WCOLS], F32R)
        kT_hi = sb("kT_hi", [P, S], F32R)
        kT_lo = sb("kT_lo", [P, S], F32R)
        v_hi = sb("v_hi", [P, T, D], F32R)
        v_lo = sb("v_lo", [P, T, D], F32R)
        angles = sb("angles", [P, 2, 2, D // 2])
        probs = sb("probs", [P, 2, 2, S])
        wo_raw = w_raw[:, 0:HG * C].rearrange("p (h n) -> p h n", n=C)
        wo_hi = sb("wo_hi", [P, HG, C], F32R)
        wo_lo = sb("wo_lo", [P, HG, C], F32R)
        qT_hi = sb("qT_hi", [P, QW], F32R)
        qT_lo = sb("qT_lo", [P, QW], F32R)
        pT_hi = sb("pT_hi", [P, PT_RING, CHUNK], F32R)
        pT_lo = sb("pT_lo", [P, PT_RING, CHUNK], F32R)
        qk_raw = sb("qk_raw", [P, HG + 1, D])
        t_same = sb("t_same", [P, HG + 1, D])
        squares = rotated = t_same
        t_swap = sb("t_swap", [P, HG + 1, D])
        table_same = sb("table_same", [P, 2, D])
        table_swap = sb("table_swap", [P, 2, D])
        table_bias = sb("table_bias", [P, 2, D])
        bias_part = t_swap[:, 0:2, :]
        gate = sb("gate", [P, 2, QW])
        oT = sb("oT", [P, QW])
        ogT_hi = sb("ogT_hi", [P, QW], F32R)
        ogT_lo = sb("ogT_lo", [P, QW], F32R)
        expert_raw = sb("expert_raw", [P, CT, C])
        fc_hi = sb("fc_hi", [P, CT, C], F32R)
        fc_lo = sb("fc_lo", [P, CT, C], F32R)
        pj_hi = sb("pj_hi", [P, CT, C], F32R)
        pj_lo = sb("pj_lo", [P, CT, C], F32R)
        hid_hi = sb("hid_hi", [P, 2, CHUNK], F32R)
        hid_lo = sb("hid_lo", [P, 2, CHUNK], F32R)
        ident_f = sb("ident_f", [P, P])
        ident_b = sb("ident_b", [P, P], BF16)
        mask_b = sb("mask_b", [P, P], BF16)
        ln_w = sb("ln_w", [P, 2, D])
        ln_b = sb("ln_b", [P, 2, D])
        ln_ws = sb("ln_ws", [P, 2, D])
        ln_bs = sb("ln_bs", [P, 2, D])
        head_sum = sb("head_sum", [P, HG + 1])
        head_mean = sb("head_mean", [P, HG + 1])
        sumsq = sb("sumsq", [P, HG + 1])
        variance = sb("variance", [P, HG + 1])
        rstd = sb("rstd", [P, HG + 1])
        minus_half = sb("minus_half", [P, T])
        neg_chunk_max = sb("neg_chunk_max", [P, 2, 2, 4])
        neg_max = sb("neg_max", [P, 2, 2])
        chunk_sum = sb("chunk_sum", [P, 2, HG, 4])
        row_sum = sb("row_sum", [P, HG])
        twice_sum = sb("twice_sum", [P, HG])
        half_inv = sb("half_inv", [P, HG])
        wr_hi = sb("wr_hi", [P, CT, E], F32R)
        wr_lo = sb("wr_lo", [P, CT, E], F32R)
        w_tok = sb("w_tok", [P, E, T])
        w_tok_g = sb("w_tok_g", [P, EG, T])
        xn = probs[:, 0, :, :].rearrange("p a (t c) -> p (a t) c", c=C)
        rt = [probs[:, 1, 0, i * T * E:(i + 1) * T * E].rearrange("p (t e) -> p t e", e=E) for i in range(4)]
        x_stats = probs[:, 1, 1, 0:T * 6].rearrange("p (t s) -> p t s", s=6)
        x_mv = probs[:, 1, 1, 128:128 + 2 * T].rearrange("p (t s) -> p t s", s=2)
        x_var = probs[:, 1, 1, 192:192 + T]
        x_rstd = probs[:, 1, 1, 224:224 + T]
        rank = probs[:, 1, 1, 256:256 + E]
        wr_raw = probs[:, 1, 1, 288:288 + CT * E].rearrange("p (a e) -> p a e", e=E)
        rs = [probs[:, 1, 1, 320 + 32 * i:320 + 32 * i + T] for i in range(6)]
        logit_T = [probs[0:E, 1, 0, CHUNK * (k + 1):CHUNK * (k + 2)] for k in range(3)] + [gate[0:E, 1, :]]
        w_raw_1 = probs[:, 1, 1, CHUNK:CHUNK + WCOLS]
        mask_f = gate[:, 0, 0:P]

        banks = [ctx.enter_context(nc.psum_tensor(f"bank{b}", [P, CHUNK], F32)) for b in range(NBANK)]
        pt_bank = [ctx.enter_context(nc.psum_tensor(f"pt_bank{b}", [P, CHUNK], F32)) for b in range(2)]
        o_bank = ctx.enter_context(nc.psum_tensor("o_bank", [P, CHUNK], F32))

        def bank(*step):
            return banks[bank_of[step]]

        x_in = [sem(f"x_in{q}") for q in range(4)]
        tables_in, consts_in, w_1_in = sem("tables_in"), sem("consts_in"), sem("w_1_in")
        stats_done, means_done, rstd_x_done = sem("stats_done"), sem("means_done"), sem("rstd_x_done")
        xn_done, xT_done = sem("xn_done"), sem("xT_done")
        xT_hi_done, xT_lo_done = sem("xT_hi_done"), sem("xT_lo_done")
        logit_T_done, logit_T_copied, logits_done = sem("logit_T_done"), sem("logit_T_copied"), sem("logits_done")
        consts_cast, wr_lo_done, pool_consts = sem("consts_cast"), sem("wr_lo_done"), sem("pool_consts")
        routing, pair_exp = sem("routing"), sem("pair_exp")
        stored = sem("stored")

        filled = Steps(sem("filled"), len(bank_of), look_back=True)
        pt_filled = Steps(sem("pt_filled"), total["turn_probs"])
        pv_done = Steps(sem("pv_done"), total["pv"], look_back=True)
        w_in_sem = Steps(sem("w_loaded"), CT, 16)
        wo_in = Steps(sem("wo_loaded"), 1, 16)
        fc_in = Steps(sem("fc_loaded"), EG, 16)
        pj_in = Steps(sem("pj_loaded"), EG, 16)
        mean_step = Steps(sem("mean_step"), 3 * CT)
        w_hi_done = Steps(sem("w_hi_done"), CT)
        w_lo_done = Steps(sem("w_lo_done"), CT)
        fc_hi_done = Steps(sem("fc_hi_done"), EG)
        fc_lo_done = Steps(sem("fc_lo_done"), EG)
        pj_hi_done = Steps(sem("pj_hi_done"), EG)
        pj_lo_done = Steps(sem("pj_lo_done"), EG)
        angles_in = [Steps(sem(f"angles_in{i}"), T // 2, 16) for i in range(2)]
        wo_hi_done = Steps(sem("wo_hi_done"), 1)
        wo_lo_done = Steps(sem("wo_lo_done"), 1)
        wtok_done = Steps(sem("wtok_done"), 1)
        qkv_read = Steps(sem("qkv_read"), 3 * T, look_back=True)
        v_lo_done = Steps(sem("v_lo_done"), T, look_back=True)
        gate_done = Steps(sem("gate_done"), T, look_back=True)
        sumsq_done = Steps(sem("sumsq_done"), T)
        variance_done = Steps(sem("variance_done"), T)
        rstd_done = Steps(sem("rstd_done"), T)
        bias_parts = Steps(sem("bias_parts"), T)
        tables_done = Steps(sem("tables_done"), T)
        same_done = Steps(sem("same_done"), T)
        swap_done = Steps(sem("swap_done"), T)
        both_done = Steps(sem("both_done"), T)
        rotated_done = Steps(sem("rotated_done"), T)
        qk_hi_done = Steps(sem("qk_hi_done"), 2 * T)
        qk_lo_done = Steps(sem("qk_lo_done"), 2 * T, look_back=True)
        n_chunks = total["scores"]
        chunk_max_done = Steps(sem("chunk_max_done"), n_many)
        neg_max_done = Steps(sem("neg_max_done"), T * HG)
        exp_done = Steps(sem("exp_done"), n_chunks, look_back=True)
        pt_hi_done = Steps(sem("pt_hi_done"), total["turn_probs"])
        pt_lo_done = Steps(sem("pt_lo_done"), total["turn_probs"], look_back=True)
        o_copied = Steps(sem("o_copied"), T * HG // 2)
        sum_step = Steps(sem("sum_step"), 2 * T)
        inv_done = Steps(sem("inv_done"), T)
        gated = Steps(sem("gated"), T)
        og_done = Steps(sem("og_done"), T, look_back=True)
        og_hi_done = Steps(sem("og_hi_done"), T)
        og_lo_done = Steps(sem("og_lo_done"), T)
        relu_done = Steps(sem("relu_done"), 2 * JOBS)
        hidden_done = Steps(sem("hidden_done"), 2 * JOBS)
        hid_hi_done = Steps(sem("hid_hi_done"), 2 * JOBS)
        hid_lo_done = Steps(sem("hid_lo_done"), 2 * JOBS, look_back=True)
        acc_done = Steps(sem("acc_done"), T + 4 * JOBS, look_back=True)

        freed_by = {
            "Q": lambda t: (qkv_read, 3 * t + 1),
            "KV": lambda t: (v_lo_done, t + 1),
            "G": lambda t: (gate_done, t + 1),
            "QT": lambda t: (qk_lo_done, 2 * t + 1),
            "KT": lambda t: (qk_lo_done, 2 * t + 2),
            "GT": lambda t: (og_done, t + 1),
            "OUT": lambda t: (acc_done, acc_number["out_add", t]),
            "scores": lambda t, h, c: (exp_done, number["exp", t, h, c]),
            "H": lambda m, d: (hid_lo_done, 2 * m + d + 1),
            "Y": lambda m, half: (acc_done, acc_number["y_add", m, half]),
        }
        acc_number, acc_before, last_add, adds = {}, {}, {}, 0
        for step in order["dve"]:
            if step[0] == "out_add":
                tiles = [step[1]]
            elif step[0] == "y_add":
                tiles = [(step[1] % 4) * 4 + 2 * step[2] + k for k in range(2)]
            else:
                continue
            for tile in tiles:
                adds += 1
                acc_before[adds] = last_add.get(tile, 0)
                last_add[tile] = adds
            acc_number[step] = adds
        last_fill = [None] * NBANK
        for step, b in bank_of.items():
            last_fill[b] = step

        def wait(eng, steps, g, n):
            eng.wait_ge(steps.sem, steps.after(g, n))

        def wait_bank_free(eng, g, *step):
            before = prior[step]
            if before is None:
                before = last_fill[bank_of[step]]
                s, n = freed_by[before[0]](*before[1:])
                eng.wait_ge(s.sem, s.after_before(g, n))
            else:
                s, n = freed_by[before[0]](*before[1:])
                wait(eng, s, g, n)

        def wait_filled_before(eng, g, n):
            eng.wait_ge(filled.sem, filled.after_before(g, n))

        def wait_filled(eng, g, *step):
            wait(eng, filled, g, number["fill", step])

        block = ctx.enter_context(nc.Block())

        @block.sync
        def _(sp):
            x_tiles = x.rearrange("(t p) c -> p t c", p=P)
            for q in range(4):
                sp.dma_start(acc[:, 4 * q:4 * q + 4, :], x_tiles[:, 4 * q:4 * q + 4, :]).then_inc(x_in[q], 16)
            sp.dma_start(ident_f[:], ident).then_inc(consts_in, 16)
            sp.dma_start(mask_f, mask).then_inc(consts_in, 16)
            sp.dma_start(wr_raw, w_router.rearrange("(a p) e -> p a e", p=P)).then_inc(consts_in, 16)
            for s in (w_in_sem, wo_in, fc_in, pj_in, *angles_in):
                sp.sem_inc(s.sem, s.first)

            def load_w(g, n):
                sp.dma_start(w_raw[:], w_in[bass.ds(g + n // CT, 1), n % CT].rearrange("o p n -> p (o n)"))\
                    .then_inc(w_in_sem.sem, 16)

            def load_expert(weights, g, n, loaded):
                sp.dma_start(expert_raw[:], weights[bass.ds(g + n // EG, 1), n % EG]
                             .rearrange("o (a p) n -> p (o a) n", p=P)).then_inc(loaded.sem, 16)

            def load_w_o(g, n):
                sp.dma_start(wo_raw, w_o[bass.ds(g + n, 1)].rearrange("o (h p) n -> p (o h) n", p=P))\
                    .then_inc(wo_in.sem, 16)

            def load_angles(t):
                sp.dma_start(angles[:, t % 2], cos_sin[(t % T) * P:(t % T + 1) * P])\
                    .then_inc(angles_in[t % 2].sem, 16)

            load_expert(w_fc, 0, 0, fc_in)
            load_w(0, 0)
            sp.dma_start(w_raw_1, w_in[0:1, 1].rearrange("o p n -> p (o n)")).then_inc(w_1_in, 16)
            for i, v in enumerate((q_w, k_w)):
                sp.dma_start(ln_w[:, i, :], v.partition_broadcast(P)).then_inc(tables_in, 16)
            for i, v in enumerate((q_b, k_b)):
                sp.dma_start(ln_b[:, i, :], v.partition_broadcast(P)).then_inc(tables_in, 16)
            load_angles(0)
            load_angles(1)
            wait(sp, w_in_sem, 0, 1)
            sp.wait_ge(w_1_in, 16)
            sp.sem_inc(w_in_sem.sem, 16)
            wait(sp, fc_lo_done, 0, 1)
            load_expert(w_proj, 0, 0, pj_in)
            wait(sp, w_lo_done, 0, 1)
            load_w_o(0, 0)
            with sp.Fori(0, KV) as g:
                for kind, n in order["sp"]:
                    if kind == "fc_load":
                        wait(sp, pj_lo_done, g, n)
                        load_expert(w_fc, g, n, fc_in)
                    elif kind == "pj_load":
                        wait(sp, fc_lo_done, g, n + 1)
                        load_expert(w_proj, g, n, pj_in)
                    elif kind == "w_load":
                        if n == 0:
                            wait(sp, wo_lo_done, g, 1)
                        else:
                            wait(sp, w_lo_done, g, CT + n)
                        load_w(g, CT + n)
                    elif kind == "wo_load":
                        wait(sp, w_lo_done, g, 2 * CT)
                        load_w_o(g, 1)
                    elif kind == "angle_load":
                        wait(sp, tables_done, g, n - 1)
                        load_angles(n)
            out_tiles = out.rearrange("(t p) c -> p t c", p=P)
            for q in range(4):
                sp.wait_ge(acc_done.sem, acc_done.after(KV - 1, max(last_add[4 * q + k] for k in range(4))))
                sp.dma_start(out_tiles[:, 4 * q:4 * q + 4, :], acc[:, 4 * q:4 * q + 4, :]).then_inc(stored, 16)
            sp.wait_ge(stored, 64)

        @block.gpsimd
        def _(pool):
            for s in (rstd_done, bias_parts, tables_done, swap_done):
                pool.sem_inc(s.sem, s.first)
            pool.memset(minus_half[:], -0.5).then_inc(pool_consts, 1)
            for e in range(E):
                pool.memset(rank[:, e:e + 1], float(E - e)).then_inc(pool_consts, 1)
            pool.wait_ge(pool_consts, 1 + E)
            for i in range(2):
                half = slice(i * T // 2, (i + 1) * T // 2)
                pool.wait_ge(means_done, (i + 1) * T // 2)
                pool.tensor_scalar(x_var[:, half], x_mv[:, half, 1], LN_EPS, None, ALU.add).then_inc(rstd_x_done, 1)
                pool.wait_ge(rstd_x_done, 2 * i + 1)
                pool.tensor_tensor(x_rstd[:, half], x_var[:, half], minus_half[:, half], ALU.pow)\
                    .then_inc(rstd_x_done, 1)
            pool.wait_ge(tables_in, 64)
            pool.tensor_scalar(ln_w[:, 0, :], ln_w[:, 0, :], D ** -0.5, None, ALU.mult).then_inc(pool_consts, 1)
            pool.tensor_scalar(ln_b[:, 0, :], ln_b[:, 0, :], D ** -0.5, None, ALU.mult).then_inc(pool_consts, 1)
            pool.wait_ge(pool_consts, 3 + E)
            for full, swapped in ((ln_w, ln_ws), (ln_b, ln_bs)):
                pool.tensor_scalar(swapped[:, :, 0:64], full[:, :, 64:128], -1.0, None, ALU.mult)
                pool.tensor_scalar(swapped[:, :, 64:128], full[:, :, 0:64], 1.0, None, ALU.mult)\
                    .then_inc(pool_consts, 1)
            pool.wait_ge(pool_consts, 5 + E)

            def halves(ap):
                return ap.rearrange("p a (b d) -> p (a b) d", b=2)

            def tables(g, t):
                cos_t = angles[:, t % 2, 0:1, :].to_broadcast([P, 4, D // 2])
                sin_t = angles[:, t % 2, 1:2, :].to_broadcast([P, 4, D // 2])
                wait(pool, angles_in[t % 2], g, t // 2 + 1)
                wait(pool, same_done, g, t)
                wait(pool, swap_done, g, t)
                wait(pool, rotated_done, g, t)
                pool.tensor_tensor(halves(table_same[:]), halves(ln_w[:]), cos_t, ALU.mult)
                pool.tensor_tensor(halves(table_swap[:]), halves(ln_ws[:]), sin_t, ALU.mult)
                pool.tensor_tensor(halves(table_bias[:]), halves(ln_b[:]), cos_t, ALU.mult)
                pool.tensor_tensor(halves(bias_part), halves(ln_bs[:]), sin_t, ALU.mult)\
                    .then_inc(bias_parts.sem, 1)
                wait(pool, bias_parts, g, t + 1)
                pool.tensor_tensor(table_bias[:], table_bias[:], bias_part, ALU.add)\
                    .then_inc(tables_done.sem, 1)

            with pool.Fori(0, KV) as g:
                for kind, t in order["pool"]:
                    if kind == "tables":
                        tables(g, t)
                    elif kind == "swap":
                        wait(pool, qkv_read, g, 3 * t + 2)
                        wait(pool, tables_done, g, t + 1)
                        for heads, i in ((slice(0, HG), 0), (slice(HG, HG + 1), 1)):
                            n = heads.stop - heads.start
                            for a, b in ((slice(0, 64), slice(64, 128)), (slice(64, 128), slice(0, 64))):
                                ins = pool.tensor_tensor(
                                    t_swap[:, heads, a], qk_raw[:, heads, b],
                                    table_swap[:, i:i + 1, a].to_broadcast([P, n, 64]), ALU.mult)
                        ins.then_inc(swap_done.sem, 1)
                    elif kind == "rstd":
                        wait(pool, variance_done, g, t + 1)
                        wait(pool, rotated_done, g, t)
                        pool.tensor_tensor(rstd[:], variance[:], minus_half[:, 0:HG + 1], ALU.pow)\
                            .then_inc(rstd_done.sem, 1)

        @block.scalar
        def _(act):
            for s in (w_hi_done, fc_hi_done, qkv_read, gate_done, qk_hi_done, exp_done, pt_hi_done,
                      o_copied, relu_done, hidden_done, hid_hi_done, gated, pj_hi_done, wo_hi_done,
                      og_hi_done):
                act.sem_inc(s.sem, s.first)
            act.wait_ge(consts_in, 48)
            act.activation(wr_hi[:], wr_raw, ACT.Copy).then_inc(consts_cast, 1)
            act.activation(ident_b[:], ident_f[:], ACT.Copy).then_inc(consts_cast, 1)
            act.activation(mask_b[:], mask_f, ACT.Copy).then_inc(consts_cast, 1)

            def w_high(g, n, raw=w_raw[:]):
                wait(act, mean_step, g, 3 * n + 3)
                act.activation(w_hi[:, n % CT, :], raw, ACT.Copy).then_inc(w_hi_done.sem, 1)

            def fc_high(g, e):
                wait(act, fc_in, g, e + 1)
                act.activation(fc_hi[:], expert_raw[:], ACT.Copy).then_inc(fc_hi_done.sem, 1)

            def proj_high(g, e):
                wait(act, pj_in, g, e + 1)
                act.activation(pj_hi[:], expert_raw[:], ACT.Copy).then_inc(pj_hi_done.sem, 1)

            def xT_high(i):
                act.wait_ge(xT_done, i + 1)
                act.activation(xT_hi[:, i % 2, (i // 2) * CHUNK:(i // 2 + 1) * CHUNK], banks[i % 4][:],
                               ACT.Copy).then_inc(xT_hi_done, 1)

            def logit_T_copy(k):
                act.wait_ge(logit_T_done, k + 1)
                act.activation(logit_T[k], pt_bank[k % 2][0:E, :], ACT.Copy).then_inc(logit_T_copied, 1)

            fc_high(0, 0)
            for i in range(4):
                xT_high(i)
            logit_T_copy(0)
            logit_T_copy(1)
            for i in range(4, 7):
                xT_high(i)
            w_high(0, 0)
            xT_high(7)
            proj_high(0, 0)
            logit_T_copy(2)
            logit_T_copy(3)
            w_high(0, 1, w_raw_1)
            act.wait_ge(routing, 10)
            act.activation(rs[3], rs[2], ACT.Exp).then_inc(pair_exp, 1)

            last_w_use = max(number["fill", (kind, T - 1)] for kind in ("Q", "KV", "G"))
            with act.Fori(0, KV) as g:
                for step in order["act"]:
                    kind, a = step[0], step[1:]
                    if kind == "w_high":
                        c = a[0]
                        if c == 0:
                            wait(act, filled, g, last_w_use)
                        w_high(g, CT + c)
                    elif kind == "fc_hi":
                        wait(act, filled, g, number["fill", ("H", 4 * a[0] - 1, 1)])
                        fc_high(g, a[0])
                    elif kind == "wo_hi":
                        wait_filled_before(act, g, number["fill", ("OUT", T - 1)])
                        wait(act, wo_in, g, 1)
                        act.activation(wo_hi[:], wo_raw, ACT.Copy).then_inc(wo_hi_done.sem, 1)
                    elif kind == "og_hi":
                        t = a[0]
                        wait(act, filled, g, number["fill", ("OUT", t - 1)] if t else 0)
                        wait(act, og_done, g, t + 1)
                        act.activation(ogT_hi[:], oT[:], ACT.Copy).then_inc(og_hi_done.sem, 1)
                    elif kind == "pj_hi":
                        wait(act, filled, g, number["fill", ("Y", 4 * a[0] - 1, 1)])
                        proj_high(g, a[0])
                    elif kind == "square":
                        m, d = a
                        wait_filled(act, g, "H", m, d)
                        act.activation(bank("H", m, d)[:], bank("H", m, d)[:], ACT.Relu).then_inc(relu_done.sem, 1)
                        wait(act, relu_done, g, 2 * m + d + 1)
                        act.activation(bank("H", m, d)[:], bank("H", m, d)[:], ACT.Square)\
                            .then_inc(hidden_done.sem, 1)
                    elif kind == "hid_hi":
                        m, d = a
                        wait(act, hidden_done, g, 2 * m + d + 1)
                        if d == 0:
                            wait(act, filled, g, number["fill", ("Y", m - 1, 1)] if m else 0)
                        act.activation(hid_hi[:, d, :], bank("H", m, d)[:], ACT.Copy).then_inc(hid_hi_done.sem, 1)
                    elif kind == "q_take":
                        t = a[0]
                        wait_filled(act, g, "Q", t)
                        wait(act, same_done, g, t)
                        wait(act, swap_done, g, t)
                        wait(act, filled, g, number["fill", ("KT", t - 1)] if t else 0)
                        act.activation(qk_raw[:, 0:HG, :], bank("Q", t)[:], ACT.Copy)
                        act.activation(squares[:, 0:HG, :], bank("Q", t)[:], ACT.Square)\
                            .then_inc(qkv_read.sem, 1)
                    elif kind == "kv_take":
                        t = a[0]
                        wait_filled(act, g, "KV", t)
                        act.activation(qk_raw[:, HG, :], bank("KV", t)[:, 0:D], ACT.Copy)
                        act.activation(squares[:, HG, :], bank("KV", t)[:, 0:D], ACT.Square)\
                            .then_inc(qkv_read.sem, 1)
                        act.activation(v_hi[:, t, :], bank("KV", t)[:, D:2 * D], ACT.Copy)\
                            .then_inc(qkv_read.sem, 1)
                    elif kind == "tanh":
                        t = a[0]
                        wait_filled(act, g, "G", t)
                        wait(act, filled, g, number["fill", ("GT", t - 2)] if t >= 2 else 0)
                        act.activation(gate[:, t % 2, :], bank("G", t)[:], ACT.Tanh, scale=0.5)\
                            .then_inc(gate_done.sem, 1)
                    elif kind == "q_hi":
                        t = a[0]
                        wait_filled(act, g, "QT", t)
                        act.activation(qT_hi[:], bank("QT", t)[:], ACT.Copy).then_inc(qk_hi_done.sem, 1)
                    elif kind == "k_hi":
                        t = a[0]
                        wait_filled(act, g, "KT", t)
                        act.activation(kT_hi[:, t * P:(t + 1) * P], bank("KT", t)[:, 0:P], ACT.Copy)\
                            .then_inc(qk_hi_done.sem, 1)
                    elif kind == "exp":
                        t, h, c = a
                        u, w = (2 * t + h // 2) % 2, chunks_of(t)[c]
                        if h % 2 == 0 and c == 0 and t:
                            wait(act, pt_filled, g, number["turn_probs", t - 1, h // 2, (t + 1) // 2 - 1])
                        if h == 0 and c == 0 and t >= 2:
                            wait(act, sum_step, g, 2 * (t - 2) + 1)
                        wait(act, neg_max_done, g, HG * t + h + 1)
                        act.activation(probs[:, u, h % 2, c * CHUNK:c * CHUNK + w], bank("scores", t, h, c)[:, 0:w],
                                       ACT.Exp, bias=neg_max[:, u, h % 2:h % 2 + 1],
                                       accum_out=chunk_sum[:, t % 2, h, c:c + 1]).then_inc(exp_done.sem, 1)
                    elif kind == "gate_scale":
                        t = a[0]
                        wait(act, inv_done, g, t + 1)
                        wait(act, gate_done, g, t + 1)
                        for h in range(HG):
                            gh, inv = gate[:, t % 2, h * D:(h + 1) * D], half_inv[:, h:h + 1]
                            ins = act.activation(gh, gh, ACT.Identity, bias=inv, scale=inv)
                        ins.then_inc(gated.sem, 1)
                    elif kind == "p_hi":
                        t, p, i = a
                        n = number[step]
                        w = 256 * min(2, t + 1 - 2 * i)
                        wait(act, pt_filled, g, n)
                        wait(act, pv_done, g, n - PT_RING)
                        act.activation(pT_hi[:, n % PT_RING, 0:w], pt_bank[n % 2][:, 0:w], ACT.Copy)\
                            .then_inc(pt_hi_done.sem, 1)
                    elif kind == "o_take":
                        t, p = a
                        wait(act, pv_done, g, number["pv", t, p, (t + 2) // 2 - 1])
                        wait(act, og_lo_done, g, t)
                        act.activation(oT[:, 256 * p:256 * p + 256], o_bank[:, 256 * p:256 * p + 256],
                                       ACT.Copy).then_inc(o_copied.sem, 1)

        @block.vector
        def _(dve):
            for s in (mean_step, variance_done, w_lo_done, fc_lo_done, wtok_done, v_lo_done, sumsq_done,
                      same_done, both_done, rotated_done, qk_lo_done, chunk_max_done, neg_max_done, pt_lo_done, sum_step, inv_done,
                      og_done, acc_done, hid_lo_done, pj_lo_done, wo_lo_done, og_lo_done):
                dve.sem_inc(s.sem, s.first)
            for t in range(T):
                dve.wait_ge(x_in[t // 4], 16)
                dve.bn_stats(x_stats[:, t, :], acc[:, t, :]).then_inc(stats_done, 1)
                if t >= 1:
                    dve.wait_ge(stats_done, t)
                    dve.bn_aggr(x_mv[:, t - 1, :], x_stats[:, t - 1, :]).then_inc(means_done, 1)
            dve.wait_ge(stats_done, T)
            dve.bn_aggr(x_mv[:, T - 1, :], x_stats[:, T - 1, :]).then_inc(means_done, 1)

            def centre(g, n, raw=w_raw[:]):
                qk = raw[:, 0:QW + D].rearrange("p (h d) -> p h d", d=D)
                wait(dve, w_in_sem, g, n + 1)
                dve.tensor_reduce(head_sum[:], qk, AX.X, ALU.add).then_inc(mean_step.sem, 1)
                wait(dve, mean_step, g, 3 * n + 1)
                dve.tensor_scalar(head_mean[:], head_sum[:], 1.0 / D, None, ALU.mult).then_inc(mean_step.sem, 1)
                wait(dve, mean_step, g, 3 * n + 2)
                dve.tensor_tensor(qk, qk, head_mean[:].unsqueeze(2).to_broadcast([P, HG + 1, D]),
                                  ALU.subtract).then_inc(mean_step.sem, 1)

            def w_low(g, n, raw=w_raw[:]):
                wait(dve, w_hi_done, g, n + 1)
                dve.tensor_tensor(w_lo[:, n % CT, :], raw, w_hi[:, n % CT, :].bitcast(F32), ALU.subtract)\
                    .then_inc(w_lo_done.sem, 1)

            def fc_low(g, e):
                wait(dve, fc_hi_done, g, e + 1)
                dve.tensor_tensor(fc_lo[:], expert_raw[:], fc_hi[:].bitcast(F32), ALU.subtract)\
                    .then_inc(fc_lo_done.sem, 1)

            def proj_low(g, e):
                wait(dve, pj_hi_done, g, e + 1)
                dve.tensor_tensor(pj_lo[:], expert_raw[:], pj_hi[:].bitcast(F32), ALU.subtract)\
                    .then_inc(pj_lo_done.sem, 1)

            def normalise(tiles):
                dve.wait_ge(rstd_x_done, 2 + 2 * (tiles[0] // (T // 2)))
                for t in tiles:
                    dve.tensor_scalar(xn[:, t, :], acc[:, t, :], x_mv[:, t, 0:1], x_rstd[:, t:t + 1],
                                      ALU.subtract, ALU.mult).then_inc(xn_done, 1)

            def xT_low(i):
                dve.wait_ge(xT_hi_done, i + 1)
                cols = slice((i // 2) * CHUNK, (i // 2 + 1) * CHUNK)
                dve.tensor_tensor(xT_lo[:, i % 2, cols], banks[i % 4][:], xT_hi[:, i % 2, cols].bitcast(F32),
                                  ALU.subtract).then_inc(xT_lo_done, 1)

            dve.wait_ge(means_done, T)
            normalise(range(T // 2))
            fc_low(0, 0)
            dve.wait_ge(consts_cast, 1)
            dve.tensor_tensor(wr_lo[:], wr_raw, wr_hi[:].bitcast(F32), ALU.subtract).then_inc(wr_lo_done, 1)
            for i in range(4):
                xT_low(i)
            normalise(range(T // 2, T))
            centre(0, 0)
            for i in range(4, 7):
                xT_low(i)
            w_low(0, 0)
            xT_low(7)
            centre(0, 1, w_raw_1)
            proj_low(0, 0)
            w_low(0, 1, w_raw_1)
            logit, pick0, rest, pick1 = rt
            top0, r_a, diff, ex, p1, p0 = rs
            done = 0

            def link(ins):
                nonlocal done
                done += 1
                ins.then_inc(routing, 1)
                dve.wait_ge(routing, done)

            def over_experts(ap):
                return ap.unsqueeze(2).to_broadcast([P, T, E])

            rank_all = rank.unsqueeze(1).to_broadcast([P, T, E])
            dve.wait_ge(logits_done, 4)
            dve.wait_ge(pool_consts, 1 + E)
            link(dve.tensor_copy(logit.rearrange("p t e -> p (t e)"), o_bank[:, 0:T * E]))
            link(dve.tensor_reduce(top0, logit, AX.X, ALU.max))
            link(dve.tensor_tensor(rest, logit, over_experts(top0), ALU.is_equal))
            link(dve.tensor_tensor(rest, rest, rank_all, ALU.mult))
            link(dve.tensor_reduce(r_a, rest, AX.X, ALU.max))
            link(dve.tensor_tensor(pick0, rank_all, over_experts(r_a), ALU.is_equal))
            link(dve.scalar_tensor_tensor(rest, pick0, MASKED, logit, ALU.mult, ALU.add))
            link(dve.tensor_reduce(r_a, rest, AX.X, ALU.max))
            link(dve.tensor_tensor(pick1, rest, over_experts(r_a), ALU.is_equal))
            link(dve.tensor_tensor(diff, r_a, top0, ALU.subtract))
            assert done == 10
            link(dve.tensor_tensor(pick1, pick1, rank_all, ALU.mult))
            link(dve.tensor_reduce(r_a, pick1, AX.X, ALU.max))
            link(dve.tensor_tensor(pick1, rank_all, over_experts(r_a), ALU.is_equal))
            dve.wait_ge(pair_exp, 1)
            link(dve.tensor_scalar(p1, ex, 1.0, None, ALU.add))
            link(dve.reciprocal(p0, p1))
            link(dve.tensor_tensor(p1, ex, p0, ALU.mult))
            link(dve.tensor_tensor(pick0, pick0, over_experts(p0), ALU.mult))
            link(dve.tensor_tensor(pick1, pick1, over_experts(p1), ALU.mult))
            link(dve.tensor_tensor(w_tok[:].rearrange("p e t -> p t e"), pick0, pick1, ALU.add))

            with dve.Fori(0, KV) as g:
                wait(dve, acc_done, g, 0)
                dve.tensor_copy(w_tok_g[:], w_tok[:, bass.ds(g * EG, EG), :]).then_inc(wtok_done.sem, 1)
                for step in order["dve"]:
                    kind, a = step[0], step[1:]
                    if kind == "centre":
                        centre(g, CT + a[0])
                    elif kind == "w_low":
                        w_low(g, CT + a[0])
                    elif kind == "fc_lo":
                        fc_low(g, a[0])
                    elif kind == "wo_lo":
                        wait(dve, wo_hi_done, g, 1)
                        dve.tensor_tensor(wo_lo[:], wo_raw, wo_hi[:].bitcast(F32), ALU.subtract)\
                            .then_inc(wo_lo_done.sem, 1)
                    elif kind == "og_lo":
                        t = a[0]
                        wait(dve, og_hi_done, g, t + 1)
                        dve.tensor_tensor(ogT_lo[:], oT[:], ogT_hi[:].bitcast(F32), ALU.subtract)\
                            .then_inc(og_lo_done.sem, 1)
                    elif kind == "pj_lo":
                        proj_low(g, a[0])
                    elif kind == "hid_lo":
                        m, d = a
                        wait(dve, hid_hi_done, g, 2 * m + d + 1)
                        dve.tensor_tensor(hid_lo[:, d, :], bank("H", m, d)[:], hid_hi[:, d, :].bitcast(F32),
                                          ALU.subtract).then_inc(hid_lo_done.sem, 1)
                    elif kind == "y_add":
                        m, half = a
                        if m == 0 and half == 0:
                            wait(dve, wtok_done, g, 1)
                        wait_filled(dve, g, "Y", m, half)
                        for k in range(2):
                            tile = (m % 4) * 4 + 2 * half + k
                            n = acc_number[step] - 1 + k
                            wait(dve, acc_done, g, acc_before[n])
                            dve.scalar_tensor_tensor(
                                acc[:, tile, :], bank("Y", m, half)[:, k * C:(k + 1) * C],
                                w_tok_g[:, m // 4, tile:tile + 1], acc[:, tile, :], ALU.mult, ALU.add)\
                                .then_inc(acc_done.sem, 1)
                    elif kind == "sumsq":
                        t = a[0]
                        wait(dve, qkv_read, g, 3 * t + 2)
                        dve.tensor_reduce(sumsq[:], squares[:], AX.X, ALU.add).then_inc(sumsq_done.sem, 1)
                        wait(dve, sumsq_done, g, t + 1)
                        dve.tensor_scalar(variance[:], sumsq[:], 1.0 / D, QK_EPS, ALU.mult, ALU.add)\
                            .then_inc(variance_done.sem, 1)
                    elif kind == "same":
                        t = a[0]
                        wait(dve, tables_done, g, t + 1)
                        wait(dve, rotated_done, g, t)
                        dve.tensor_tensor(t_same[:, HG, :], qk_raw[:, HG, :], table_same[:, 1, :], ALU.mult)
                        dve.tensor_tensor(t_same[:, 0:HG, :], qk_raw[:, 0:HG, :],
                                          table_same[:, 0:1, :].to_broadcast([P, HG, D]), ALU.mult)\
                            .then_inc(same_done.sem, 1)
                    elif kind == "v_lo":
                        t = a[0]
                        wait(dve, qkv_read, g, 3 * t + 3)
                        dve.tensor_tensor(v_lo[:, t, :], bank("KV", t)[:, D:2 * D], v_hi[:, t, :].bitcast(F32),
                                          ALU.subtract).then_inc(v_lo_done.sem, 1)
                    elif kind == "rope_b":
                        t = a[0]
                        wait(dve, swap_done, g, t + 1)
                        wait(dve, same_done, g, t + 1)
                        dve.tensor_tensor(t_same[:], t_same[:], t_swap[:], ALU.add).then_inc(both_done.sem, 1)
                        wait(dve, both_done, g, t + 1)
                        wait(dve, rstd_done, g, t + 1)
                        for h in range(HG + 1):
                            ins = dve.scalar_tensor_tensor(rotated[:, h, :], t_same[:, h, :], rstd[:, h:h + 1],
                                                           table_bias[:, h // HG, :], ALU.mult, ALU.add)
                        ins.then_inc(rotated_done.sem, 1)
                    elif kind == "q_lo":
                        t = a[0]
                        wait(dve, qk_hi_done, g, 2 * t + 1)
                        dve.tensor_tensor(qT_lo[:], bank("QT", t)[:], qT_hi[:].bitcast(F32), ALU.subtract)\
                            .then_inc(qk_lo_done.sem, 1)
                    elif kind == "k_lo":
                        t = a[0]
                        wait(dve, qk_hi_done, g, 2 * t + 2)
                        cols = slice(t * P, (t + 1) * P)
                        dve.tensor_tensor(kT_lo[:, cols], bank("KT", t)[:, 0:P], kT_hi[:, cols].bitcast(F32),
                                          ALU.subtract).then_inc(qk_lo_done.sem, 1)
                    elif kind == "max":
                        t, h, c = a
                        u, w, n = (2 * t + h // 2) % 2, chunks_of(t)[c], len(chunks_of(t))
                        if c == 0 and t:
                            wait(dve, exp_done, g, number["exp", t - 1, h, len(chunks_of(t - 1)) - 1])
                        wait_filled(dve, g, "scores", t, h, c)
                        nm = neg_max[:, u, h % 2:h % 2 + 1]
                        if n == 1:
                            dve.tensor_reduce(nm, bank("scores", t, h, c)[:, 0:w], AX.X, ALU.max, negate=True)\
                                .then_inc(neg_max_done.sem, 1)
                        else:
                            dve.tensor_reduce(neg_chunk_max[:, u, h % 2, c:c + 1], bank("scores", t, h, c)[:, 0:w],
                                              AX.X, ALU.max, negate=True).then_inc(chunk_max_done.sem, 1)
                            if c == n - 1:
                                wait(dve, chunk_max_done, g, number[step] - (total["scores"] - n_many))
                                dve.tensor_reduce(nm, neg_chunk_max[:, u, h % 2, 0:n], AX.X, ALU.min)\
                                    .then_inc(neg_max_done.sem, 1)
                    elif kind == "p_lo":
                        t, p, i = a
                        n = number[step]
                        w = 256 * min(2, t + 1 - 2 * i)
                        wait(dve, pt_hi_done, g, n)
                        dve.tensor_tensor(pT_lo[:, n % PT_RING, 0:w], pt_bank[n % 2][:, 0:w],
                                          pT_hi[:, n % PT_RING, 0:w].bitcast(F32), ALU.subtract)\
                            .then_inc(pt_lo_done.sem, 1)
                    elif kind == "inv":
                        t = a[0]
                        n = len(chunks_of(t))
                        wait(dve, exp_done, g, number["exp", t, HG - 1, n - 1])
                        dve.tensor_reduce(row_sum[:], chunk_sum[:, t % 2, :, 0:n], AX.X, ALU.add)\
                            .then_inc(sum_step.sem, 1)
                        wait(dve, sum_step, g, 2 * t + 1)
                        dve.tensor_scalar(twice_sum[:], row_sum[:], 2.0, None, ALU.mult).then_inc(sum_step.sem, 1)
                        wait(dve, sum_step, g, 2 * t + 2)
                        wait(dve, gated, g, t)
                        dve.reciprocal(half_inv[:], twice_sum[:]).then_inc(inv_done.sem, 1)
                    elif kind == "og":
                        t = a[0]
                        wait_filled(dve, g, "GT", t)
                        wait(dve, o_copied, g, 2 * t + 2)
                        dve.tensor_tensor(oT[:], bank("GT", t)[:], oT[:], ALU.mult)\
                            .then_inc(og_done.sem, 1)
                    elif kind == "out_add":
                        t = a[0]
                        wait_filled(dve, g, "OUT", t)
                        n = acc_number[step]
                        wait(dve, acc_done, g, acc_before[n])
                        dve.tensor_tensor(acc[:, t, :], bank("OUT", t)[:, 0:C], acc[:, t, :], ALU.add)\
                            .then_inc(acc_done.sem, 1)

        @block.tensor
        def _(pe):
            for s in (filled, pt_filled, pv_done):
                pe.sem_inc(s.sem, s.first)
            pe.wait_ge(consts_in, 48)

            def logits(k):
                pe.wait_ge(xT_lo_done, 2 * k + 2)
                if k == 0:
                    pe.wait_ge(wr_lo_done, 1)
                if k >= 2:
                    pe.wait_ge(logit_T_copied, k - 1)
                cols = slice(k * CHUNK, (k + 1) * CHUNK)
                todo = [(ws, xs, c) for c in range(CT) for ws, xs in
                        ((wr_hi, xT_hi), (wr_lo, xT_hi), (wr_hi, xT_lo))]
                for n, (ws, xs, c) in enumerate(todo):
                    ins = pe.matmul(pt_bank[k % 2][0:E, :], ws[:, c, :], xs[:, c, cols],
                                    start=(n == 0), stop=(n == len(todo) - 1))
                ins.then_inc(logit_T_done, 1)

            def turn_logits(k):
                pe.wait_ge(logit_T_copied, k + 1)
                for i in range(4):
                    t = 4 * k + i
                    ins = pe.transpose(o_bank[:, t * E:(t + 1) * E], logit_T[k][:, i * P:(i + 1) * P],
                                       ident_f[0:E, 0:E])
                ins.then_inc(logits_done, 1)

            def turn_x(i):
                if i >= 4:
                    pe.wait_ge(xT_lo_done, i - 3)
                for k in range(4):
                    t = 4 * (i // 2) + k
                    pe.wait_ge(xn_done, t + 1)
                    ins = pe.transpose(banks[i % 4][:, k * P:(k + 1) * P], xn[:, t, (i % 2) * P:(i % 2 + 1) * P],
                                       ident_f[:])
                ins.then_inc(xT_done, 1)

            for i in range(4):
                turn_x(i)
            logits(0)
            logits(1)
            turn_x(4)
            turn_x(5)
            turn_logits(0)
            turn_x(6)
            turn_x(7)
            turn_logits(1)
            logits(2)
            logits(3)
            turn_logits(2)
            turn_logits(3)
            pe.wait_ge(consts_cast, 3)

            def three(out_ap, stationary, moving, start=True, stop=True):
                n, last = len(stationary), 3 * len(stationary)
                done = 0
                for (s_hi, s_lo), (m_hi, m_lo) in zip(stationary, moving):
                    for s, m in ((s_hi, m_hi), (s_hi, m_lo), (s_lo, m_hi)):
                        done += 1
                        ins = pe.matmul(out_ap, s, m, start=(start and done == 1), stop=(stop and done == last))
                return ins

            with pe.Fori(0, KV) as g:
                for step in order["pe"]:
                    kind, a = step[0], step[1:]
                    if kind in FILLS:
                        wait_bank_free(pe, g, *step)
                    if kind == "H":
                        m, d = a
                        cols, ds = slice((m % 4) * CHUNK, (m % 4 + 1) * CHUNK), slice(d * P, (d + 1) * P)
                        if m % 4 == 0 and d == 0:
                            wait(pe, fc_lo_done, g, m // 4 + 1)
                        three(bank("H", m, d)[:], [(fc_hi[:, c, ds], fc_lo[:, c, ds]) for c in range(CT)],
                              [(xT_hi[:, c, cols], xT_lo[:, c, cols]) for c in range(CT)])\
                            .then_inc(filled.sem, 1)
                    elif kind == "Y":
                        m, half = a
                        if m % 4 == 0 and half == 0:
                            wait(pe, pj_lo_done, g, m // 4 + 1)
                        wait(pe, hid_lo_done, g, 2 * m + 2)
                        for k in range(2):
                            cols = slice((2 * half + k) * P, (2 * half + k + 1) * P)
                            ins = three(bank("Y", m, half)[:, k * C:(k + 1) * C],
                                        [(hid_hi[:, d, cols], hid_lo[:, d, cols]) for d in range(2)],
                                        [(pj_hi[:, d, :], pj_lo[:, d, :]) for d in range(2)])
                        ins.then_inc(filled.sem, 1)
                    elif kind in ("Q", "KV", "G"):
                        t = a[0]
                        rows = slice(t * P, (t + 1) * P)
                        cols = {"Q": slice(0, QW), "KV": slice(QW, QW + 2 * D), "G": slice(QW + 2 * D, WCOLS)}[kind]
                        if t == 0 and kind == "Q":
                            wait(pe, w_lo_done, g, CT)
                        three(bank(kind, t)[:, 0:cols.stop - cols.start],
                              [(xT_hi[:, c, rows], xT_lo[:, c, rows]) for c in range(CT)],
                              [(w_hi[:, c, cols], w_lo[:, c, cols]) for c in range(CT)]).then_inc(filled.sem, 1)
                    elif kind == "QT":
                        t = a[0]
                        wait(pe, rotated_done, g, t + 1)
                        for h in range(HG):
                            ins = pe.transpose(bank("QT", t)[:, h * P:(h + 1) * P], rotated[:, h, :], ident_f[:])
                        ins.then_inc(filled.sem, 1)
                    elif kind == "KT":
                        t = a[0]
                        pe.transpose(bank("KT", t)[:, 0:P], rotated[:, HG, :], ident_f[:]).then_inc(filled.sem, 1)
                    elif kind == "scores":
                        t, h, c = a
                        w = chunks_of(t)[c]
                        if h == 0 and c == 0:
                            wait(pe, qk_lo_done, g, 2 * t + 2)
                        heads, keys = slice(h * P, (h + 1) * P), slice(c * CHUNK, c * CHUNK + w)
                        diagonal = c == len(chunks_of(t)) - 1
                        ins = three(bank("scores", t, h, c)[:, 0:w],
                                    [(qT_hi[:, heads], qT_lo[:, heads])],
                                    [(kT_hi[:, keys], kT_lo[:, keys])], stop=not diagonal)
                        if diagonal:
                            ins = pe.matmul(bank("scores", t, h, c)[:, w - P:w], ident_b[:], mask_b[:],
                                            start=False, stop=True)
                        ins.then_inc(filled.sem, 1)
                    elif kind == "turn_probs":
                        t, p, i = a
                        n = number[step]
                        wait(pe, exp_done, g, max(number["exp", t, 2 * p + hh, min(2 * i + 1, t) // 4]
                                                  for hh in range(2)))
                        wait(pe, pt_lo_done, g, n - 2)
                        for jj in range(min(2, t + 1 - 2 * i)):
                            for hh in range(2):
                                j = 2 * i + jj
                                ins = pe.transpose(pt_bank[n % 2][:, (2 * jj + hh) * P:(2 * jj + hh + 1) * P],
                                                   probs[:, (2 * t + p) % 2, hh, j * P:(j + 1) * P], ident_f[:])
                        ins.then_inc(pt_filled.sem, 1)
                    elif kind == "pv":
                        t, p, i = a
                        n = number[step]
                        wait(pe, pt_lo_done, g, n)
                        if i == 0:
                            wait(pe, o_copied, g, 2 * t + p)
                            wait(pe, v_lo_done, g, t + 1)
                        for jj in range(min(2, t + 1 - 2 * i)):
                            j, cols = 2 * i + jj, slice(2 * jj * P, 2 * (jj + 1) * P)
                            ins = three(o_bank[:, 256 * p:256 * p + 256], [(v_hi[:, j, :], v_lo[:, j, :])],
                                        [(pT_hi[:, n % PT_RING, cols], pT_lo[:, n % PT_RING, cols])],
                                        start=(j == 0), stop=(j == t))
                        ins.then_inc(pv_done.sem, 1)
                    elif kind == "GT":
                        t = a[0]
                        wait(pe, gated, g, t + 1)
                        for h in range(HG):
                            ins = pe.transpose(bank("GT", t)[:, h * P:(h + 1) * P],
                                               gate[:, t % 2, h * D:(h + 1) * D], ident_f[:])
                        ins.then_inc(filled.sem, 1)
                    elif kind == "OUT":
                        t = a[0]
                        wait(pe, og_lo_done, g, t + 1)
                        if t == 0:
                            wait(pe, wo_lo_done, g, 1)
                        heads = [slice(h * P, (h + 1) * P) for h in range(HG)]
                        three(bank("OUT", t)[:, 0:C], [(ogT_hi[:, cols], ogT_lo[:, cols]) for cols in heads],
                              [(wo_hi[:, h, :], wo_lo[:, h, :]) for h in range(HG)]).then_inc(filled.sem, 1)


def kernel(L0_attn_x, L0_attn_w_qkv, L0_attn_w_o, L0_attn_q_norm_w, L0_attn_q_norm_b, L0_attn_k_norm_w,
           L0_attn_k_norm_b, L0_ffn_w_router, L0_ffn_w_fc, L0_ffn_w_proj):
    import concourse.bacc as bacc
    from concourse.bass_utils import run_bass_kernel_spmd

    pairs = np.concatenate([np.arange(0, D, 2), np.arange(1, D, 2)])
    w = np.asarray(L0_attn_w_qkv)
    wq = w[0:H * D].reshape(KV, HG, D, C)[:, :, pairs].reshape(KV, HG * D, C)
    wg = w[H * D:2 * H * D].reshape(KV, HG * D, C)
    wk = w[2 * H * D:2 * H * D + KV * D].reshape(KV, D, C)[:, pairs]
    wv = w[2 * H * D + KV * D:].reshape(KV, D, C)
    w_in = np.concatenate([wq, wk, wv, wg], axis=1).transpose(0, 2, 1).reshape(KV, CT, P, WCOLS)
    inv = np.float32(1.0) / np.power(np.float32(ROPE_BASE), np.arange(0, D, 2, dtype=np.float32) / np.float32(D))
    angles = np.outer(np.arange(S, dtype=np.float32), inv.astype(np.float32)).astype(np.float32)
    def and_first(groups):
        return np.concatenate([groups, groups[0:1]])

    arrays = {
        "x": np.asarray(L0_attn_x).reshape(S, C),
        "w_in": and_first(w_in),
        "w_o": and_first(np.asarray(L0_attn_w_o).T.reshape(KV, HG * D, C)),
        "q_w": np.asarray(L0_attn_q_norm_w)[pairs],
        "q_b": np.asarray(L0_attn_q_norm_b)[pairs],
        "k_w": np.asarray(L0_attn_k_norm_w)[pairs],
        "k_b": np.asarray(L0_attn_k_norm_b)[pairs],
        "w_router": np.asarray(L0_ffn_w_router),
        "w_fc": and_first(np.asarray(L0_ffn_w_fc).reshape(KV, EG, C, C)),
        "w_proj": and_first(np.asarray(L0_ffn_w_proj).reshape(KV, EG, C, C)),
        "cos_sin": np.stack([np.cos(angles), np.sin(angles)], axis=1),
        "ident": np.eye(P, dtype=np.float32),
        "mask": np.triu(np.full((P, P), MASKED, np.float32), 1),
    }
    arrays = {n: np.ascontiguousarray(a) for n, a in arrays.items()}
    nc = bacc.Bacc("TRN2", target_bir_lowering=False, num_devices=1)
    args = [nc.dram_tensor(f"in_{n}", a.shape, mybir.dt.from_np(a.dtype), kind="ExternalInput").ap()
            for n, a in arrays.items()]
    args.append(nc.dram_tensor("out_0", (S, C), F32, kind="ExternalOutput").ap())
    build(nc, *args)
    r = run_bass_kernel_spmd(nc, [{f"in_{n}": a for n, a in arrays.items()}], core_ids=[0])
    return r.results[0]["out_0"].reshape(1, S, C)
```
